# Optimizing a Trainium2 kernel written in Bass

```python
import numpy as np
import jax
import jax.numpy as jnp

def _softmax(x, axis=-1):
    return jax.nn.softmax(x, axis=axis)

def _gelu(x):
    return jax.nn.gelu(x, approximate=True)

def _silu(x):
    return jax.nn.silu(x)

def _sigmoid(x):
    return jax.nn.sigmoid(x)

def _layernorm(x, axis=-1, eps=1e-05):
    m = jnp.mean(x, axis=axis, keepdims=True)
    v = jnp.var(x, axis=axis, keepdims=True)
    return (x - m) / jnp.sqrt(v + eps)

def _scatter_add(tgt, idx, src, axis=0):
    return tgt.at[idx].add(src)

def _segment_sum(src, seg, n):
    return jax.ops.segment_sum(src, seg, n)
kernel_name = 'mk_sandwich_d1_jaxref_r4_fd27de'

def setup_inputs(seed: int=0):
    np.random.seed(seed)
    _w = jnp.asarray

    def _L0_attn_setup():
        import jax, jax.numpy as jnp
        import numpy as np
        key = jax.random.key(seed)
        k1, k2, k3 = jax.random.split(key, 3)
        B, L, D = (8, 1024, 256)
        s = 1.0 / np.sqrt(D)
        return {'x': jax.random.normal(k1, (B, L, D), dtype=jnp.float32), 'Wg': jax.random.normal(k2, (D, D), dtype=jnp.float32) * s, 'bg': jnp.zeros((D,), dtype=jnp.float32), 'Wo': jax.random.normal(k3, (D, D), dtype=jnp.float32) * s, 'bo': jnp.zeros((D,), dtype=jnp.float32)}
    _L0_attn_in = _L0_attn_setup()

    def _L0_ffn_setup():
        import jax, jax.numpy as jnp
        import numpy as np
        E = 8
        C = 320
        D = 256
        H = 1024
        B, S = (4, 512)
        key = jax.random.key(seed)
        ks = jax.random.split(key, 12)
        sc = 0.02
        return {'input': jax.random.normal(ks[0], (B, S, D), jnp.float32), 'router_w': jax.random.normal(ks[1], (D, E), jnp.float32) * sc, 'router_b': jnp.zeros((E,), jnp.float32), 'w1': jax.random.normal(ks[2], (E, D, H), jnp.float32) * sc, 'b1': jnp.zeros((E, H), jnp.float32), 'w2': jax.random.normal(ks[3], (E, H, D), jnp.float32) * sc, 'b2': jnp.zeros((E, D), jnp.float32), 'ow1': jax.random.normal(ks[4], (D, H), jnp.float32) * sc, 'ob1': jnp.zeros((H,), jnp.float32), 'ow2': jax.random.normal(ks[5], (H, D), jnp.float32) * sc, 'ob2': jnp.zeros((D,), jnp.float32)}
    _L0_ffn_in = _L0_ffn_setup()
    _d = {'L0_attn_x': _L0_attn_in['x'], 'L0_attn_Wg': _L0_attn_in['Wg'], 'L0_attn_bg': _L0_attn_in['bg'], 'L0_attn_Wo': _L0_attn_in['Wo'], 'L0_attn_bo': _L0_attn_in['bo'], 'L0_ffn_router_w': _L0_ffn_in['router_w'], 'L0_ffn_router_b': _L0_ffn_in['router_b'], 'L0_ffn_w1': _L0_ffn_in['w1'], 'L0_ffn_b1': _L0_ffn_in['b1'], 'L0_ffn_w2': _L0_ffn_in['w2'], 'L0_ffn_b2': _L0_ffn_in['b2'], 'L0_ffn_ow1': _L0_ffn_in['ow1'], 'L0_ffn_ob1': _L0_ffn_in['ob1'], 'L0_ffn_ow2': _L0_ffn_in['ow2'], 'L0_ffn_ob2': _L0_ffn_in['ob2']}
    _x0 = _d['L0_attn_x']
    _d['L0_attn_x'] = jax.random.normal(jax.random.fold_in(jax.random.key(seed), 1), (16, 1024, 256), dtype=_x0.dtype)
    del _x0
    return _d

def reference(L0_attn_x, L0_attn_Wg, L0_attn_bg, L0_attn_Wo, L0_attn_bo, L0_ffn_router_w, L0_ffn_router_b, L0_ffn_w1, L0_ffn_b1, L0_ffn_w2, L0_ffn_b2, L0_ffn_ow1, L0_ffn_ob1, L0_ffn_ow2, L0_ffn_ob2):

    def _L0_attn_ref(x, Wg, bg, Wo, bo):
        import jax, jax.numpy as jnp
        import numpy as np
        g = jax.nn.sigmoid(jnp.einsum('bld,ed->ble', x, Wg) + bg)
        a = 1.0 - g
        b = g * x

        def combine(c1, c2):
            a1, b1 = c1
            a2, b2 = c2
            return (a2 * a1, a2 * b1 + b2)
        _, h = jax.lax.associative_scan(combine, (a, b), axis=1)
        return jnp.einsum('bld,ed->ble', h, Wo) + bo

    def _L0_ffn_ref(input, router_w, router_b, w1, b1, w2, b2, ow1, ob1, ow2, ob2):
        import jax, jax.numpy as jnp
        import numpy as np
        E = 8
        C = 320
        D = 256
        H = 1024
        B, S = (4, 512)
        Bq, Sq, Dq = input.shape
        N = Bq * Sq
        xf = input.reshape(N, Dq)
        probs = jax.nn.softmax(xf @ router_w + router_b, axis=-1)
        eid = jnp.argmax(probs, axis=-1)
        onehot = jax.nn.one_hot(eid, E, dtype=xf.dtype)
        rank = (jnp.cumsum(onehot, axis=0)[jnp.arange(N), eid] - 1.0).astype(jnp.int32)
        valid = rank < C
        pos = jnp.where(valid, rank, 0)
        vmask = valid.astype(xf.dtype)[:, None]
        buf = jnp.zeros((E, C, Dq), xf.dtype).at[eid, pos].add(xf * vmask)
        h = jax.nn.relu(jnp.einsum('ecd,edh->ech', buf, w1) + b1[:, None, :])
        y = jnp.einsum('ech,ehd->ecd', h, w2) + b2[:, None, :]
        y_tok = y[eid, pos] * vmask
        yov = jax.nn.relu(xf @ ow1 + ob1) @ ow2 + ob2
        out = y_tok + yov * (1.0 - vmask)
        return out.reshape(Bq, Sq, Dq)
    x = L0_attn_x
    x = x + _layernorm(_L0_attn_ref(_layernorm(x, axis=-1), L0_attn_Wg, L0_attn_bg, L0_attn_Wo, L0_attn_bo), axis=-1)
    x = x + _layernorm(_L0_ffn_ref(_layernorm(x, axis=-1), L0_ffn_router_w, L0_ffn_router_b, L0_ffn_w1, L0_ffn_b1, L0_ffn_w2, L0_ffn_b2, L0_ffn_ow1, L0_ffn_ob1, L0_ffn_ow2, L0_ffn_ob2), axis=-1)
    return x

_drawn_inputs = setup_inputs


def setup_inputs(seed=0):
    import zlib

    import numpy as np

    out = dict(_drawn_inputs(seed))
    spreads = {'L0_attn_bg': (0.0, 0.1),
     'L0_attn_bo': (0.0, 0.1),
     'L0_ffn_router_b': (0.0, 0.1),
     'L0_ffn_b1': (0.0, 0.1),
     'L0_ffn_b2': (0.0, 0.1),
     'L0_ffn_ob1': (0.0, 0.1),
     'L0_ffn_ob2': (0.0, 0.1)}
    factors = {}
    for name, (base, spread) in spreads.items():
        noise = np.random.default_rng([zlib.crc32(name.encode()), seed]).standard_normal(out[name].shape)
        drawn = base * np.exp(spread * noise) if base else spread * noise
        out[name] = jnp.asarray(drawn.astype(out[name].dtype))
    for name, factor in factors.items():
        out[name] = (out[name] * factor).astype(out[name].dtype)
    return out
```

```python
from contextlib import ExitStack

import concourse.bass as bass
from concourse import mybir

ALU = mybir.AluOpType
ACT = mybir.ActivationFunctionType
F32 = mybir.dt.float32
F32R = mybir.dt.float32r
BF16 = mybir.dt.bfloat16
I32 = mybir.dt.int32
AX_X = mybir.AxisListType.X

P = 128
D = 256
DC = D // P
H = 1024
HC = H // P
E = 8
C = 320
TG = 4
GT = TG * P
ROW = D + 1
PITCH = 260
ET = -(-C // P)
EPS = 1e-5
NOWHERE = 1.0e6
TIE = 2.0 ** -25


def grp(i, u, k):
    return i + (u + k) // 2, (u + k) % 2


def cnt(g, n, k):
    return g[0] * (2 * n) + (g[1] * n + k)


def landed(g, n=1):
    return g[0] * (16 * n) + 16 * n


def live(g, n):
    return not isinstance(g[0], int) or 0 <= 2 * g[0] + g[1] < n


def sandwich_kernel(nc, x, Wg, bg, Wo, bo, router_w, router_b, w1, b1, w2, b2, ow1, ob1, ow2, ob2, out):
    B, L, _ = x.shape
    N = B * L
    NG = N // GT
    assert L == 2 * GT and Wg.shape == (D, D) and w1.shape == (E, D, H)
    out_rows = out.rearrange("b l d -> (b l) d")

    with ExitStack() as ctx:
        def sb(name, shape, dt=F32):
            return ctx.enter_context(nc.sbuf_tensor(name, shape, dt))

        def sem(name):
            return ctx.enter_context(nc.semaphore(name))

        def sems(name):
            return [sem(f"{name}{v}") for v in range(2)]

        xbuf = nc.dram_tensor("xbuf", [E * C, ROW], F32).ap()

        stage = sb("stage", [P, 2, 2048])
        WgT = [sb(f"WgT_{p}", [P, DC, D], F32R) for p in ("hi", "lo")]
        WoT = [sb(f"WoT_{p}", [P, DC, D], F32R) for p in ("hi", "lo")]
        rw = sb("rw", [P, DC, 2 * E], F32R)
        rw_raw = sb("rw_raw", [P, DC, E])
        W1 = [[sb(f"W1_{p}{v}", [P, DC, H], F32R) for p in ("hi", "lo")] for v in range(2)]
        W2 = [[sb(f"W2_{p}{v}", [P, HC, D], F32R) for p in ("hi", "lo")] for v in range(2)]
        bias_rows = sb("bias_rows", [P, P])
        biasT = sb("biasT", [P, P])
        neg_bg = sb("neg_bg", [P, DC])
        bo_b = sb("bo_b", [P, D])
        ob2_b = sb("ob2_b", [P, D])
        b2_b = sb("b2_b", [P, E, D])
        rb_b = sb("rb_b", [P, E])
        OB1 = E * HC
        BG = OB1 + HC

        ident = sb("ident", [P, P])
        upto = sb("upto", [P, P], BF16)
        ones = sb("ones", [P, P], BF16)
        first = sb("first", [P, E])
        row0 = sb("row0", [P, E])
        mhalf = sb("mhalf", [P, TG])
        zrow = sb("zrow", [P, ROW])
        id_int = sb("id_int", [P, 2, TG], I32)

        xin = [sb(f"xin{v}", [P, TG, D]) for v in range(2)]
        xe = [xin[v][:].rearrange("p t d -> p (t d)")[:, 0:ET * PITCH].rearrange("p (t d) -> p t d", d=PITCH)
              for v in range(2)]
        tok = sb("tok", [P, TG, D])
        xnT = sb("xnT", [P, DC, GT])
        xnT_hi = sb("xnT_hi", [P, DC, GT], F32R)
        xnT_lo = sb("xnT_lo", [P, DC, GT], F32R)
        keep = sb("keep", [P, DC, GT])
        hst = [sb(f"hst{v}", [P, DC, GT]) for v in range(2)]
        hst_hi = sb("hst_hi", [P, DC, GT], F32R)
        hst_lo = sb("hst_lo", [P, DC, GT], F32R)
        att = sb("att", [P, TG, D])
        x1 = [sb(f"x1_{v}", [P, TG, PITCH]) for v in range(2)]
        tok2 = sb("tok2", [P, TG, D])
        xfT_hi = sb("xfT_hi", [P, DC, GT], F32R)
        xfT_lo = sb("xfT_lo", [P, DC, GT], F32R)
        hid = [sb(f"hid{v}", [P, GT]) for v in range(2)]
        hid_hi = [sb(f"hid_hi{r}", [P, GT], F32R) for r in range(4)]
        hid_lo = [sb(f"hid_lo{r}", [P, GT], F32R) for r in range(4)]
        ysb = sb("ysb", [P, TG, D])
        outt = [sb(f"outt{v}", [P, TG, D]) for v in range(2)]

        st = [sb(f"st{k}", [P, TG, 6]) for k in range(4)]
        mv = [sb(f"mv{k}", [P, TG, 2]) for k in range(4)]
        veps = [sb(f"veps{k}", [P, TG]) for k in range(4)]
        nmean = [sb(f"nmean{k}", [P, TG]) for k in range(4)]
        rstd = [sb(f"rstd{k}", [P, TG]) for k in range(4)]
        nmr = [sb(f"nmr{k}", [P, TG]) for k in range(4)]

        lg = [sb(f"lg{k}", [P, TG, E]) for k in range(3)]
        lmax = sb("lmax", [P, TG])
        cand = sb("cand", [P, TG, E])
        cmax = sb("cmax", [P, TG])
        oh = sb("oh", [P, TG, E], BF16)
        seen = sb("seen", [P, E], BF16)
        seen_g = sb("seen_g", [P, E])
        rk = [sb(f"rk{k}", [P, TG, E]) for k in range(4)]
        slot = sb("slot", [P, TG])
        idx = [sb(f"idx{v}", [P, TG], I32) for v in range(2)]
        oidx = [sb(f"oidx{v}", [P, ET], I32) for v in range(2)]

        psT = ctx.enter_context(nc.psum_tensor("psT", [P, DC, GT], F32))
        psA = ctx.enter_context(nc.psum_tensor("psA", [P, 2, GT], F32))
        psH = ctx.enter_context(nc.psum_tensor("psH", [P, 2, GT], F32))
        psY = ctx.enter_context(nc.psum_tensor("psY", [P, 2, GT], F32))
        psA_t = psA[:].rearrange("p a (t d) -> p (a t) d", d=D)
        psY_t = psY[:].rearrange("p a (t d) -> p (a t) d", d=D)
        logits = psT[:, 0, 0:TG * 2 * E].rearrange("p (t e) -> p t e", t=TG)
        ranks = psT[:, 1, 0:TG * E].rearrange("p (t e) -> p t e", t=TG)

        s_x_in = sems("s_x_in")
        s_xbuf0 = sem("s_xbuf0")
        s_w = {n: sem(f"s_w_{n}") for n in ("wg", "wo", "rw", "ow", "bias", "bcast")}
        s_const = sem("s_const")
        s_held = sem("s_held")
        s_held_v = sem("s_held_v")
        s_pc = sem("s_pc")
        s_id = sem("s_id")
        s_bias_z = sem("s_bias_z")
        s_wT = sem("s_wT")
        s_wT_hi = sem("s_wT_hi")
        s_wT_lo = sem("s_wT_lo")
        s_rw_hi = sem("s_rw_hi")
        s_rw_lo = sem("s_rw_lo")
        s_ow_hi = sem("s_ow_hi")
        s_ow_lo = sem("s_ow_lo")
        s_biasT = sem("s_biasT")
        s_st = [sem(f"s_st{k}") for k in range(4)]
        s_ag = [sem(f"s_ag{k}") for k in range(4)]
        s_ve = [sem(f"s_ve{k}") for k in range(4)]
        s_rs = [sem(f"s_rs{k}") for k in range(4)]
        s_nm = [sem(f"s_nm{k}") for k in range(4)]
        s_tok = sem("s_tok")
        s_T0 = sem("s_T0")
        s_xn_hi = sem("s_xn_hi")
        s_xn_lo = sem("s_xn_lo")
        s_gate = sem("s_gate")
        s_keep = sem("s_keep")
        s_ngx = sem("s_ngx")
        s_scan = sem("s_scan")
        s_h_hi = sem("s_h_hi")
        s_h_lo = sem("s_h_lo")
        s_wo = sem("s_wo")
        s_att = sem("s_att")
        s_u = sem("s_u")
        s_x1 = sem("s_x1")
        s_tok2 = sem("s_tok2")
        s_T1 = sem("s_T1")
        s_xf_hi = sem("s_xf_hi")
        s_xf_lo = sem("s_xf_lo")
        s_lg = sem("s_lg")
        s_rt = sem("s_rt")
        s_oh = sem("s_oh")
        s_rank = sem("s_rank")
        s_sl = sem("s_sl")
        s_idx = sem("s_idx")
        s_seen = sem("s_seen")
        s_scat = sems("s_scat")
        s_l1 = sem("s_l1")
        s_hid = sem("s_hid")
        s_hid_hi = sem("s_hid_hi")
        s_hid_lo = sem("s_hid_lo")
        s_l2 = sem("s_l2")
        s_y = sem("s_y")
        s_z = sem("s_z")
        s_out = sem("s_out")
        s_st_out = sems("s_st_out")
        s_we = [sems(f"s_we{m}_") for m in (1, 2)]
        s_we_hi = sem("s_we_hi")
        s_we_lo = sem("s_we_lo")
        s_xe = sems("s_xe")
        s_oidx = sem("s_oidx")
        s_fin = sems("s_fin")

        EL1, EST = cnt((NG // 2, 0), HC, 0), NG

        block = ctx.enter_context(nc.Block())

        def stage_w1():
            return stage[:, 0, :].rearrange("p (c h) -> p c h", c=DC)

        def stage_w2():
            return stage[:, 1, :].rearrange("p (c d) -> p c d", c=HC)

        @block.sync
        def _(sp):
            def load(g):
                i, v = g
                sp.dma_start(xin[v][:], x[i, v * GT:(v + 1) * GT, :].rearrange("(t p) d -> p t d", p=P))\
                    .then_inc(s_x_in[v], 16)

            load((0, 0))
            wg_raw = outt[0][:, 0:DC, :]
            wo_raw = outt[1][:, 0:DC, :]
            sp.dma_start(wg_raw, Wg.rearrange("(c p) d -> p c d", p=P)).then_inc(s_w["wg"], 16)
            sp.wait_ge(s_bias_z, 1)
            sp.dma_start(bias_rows[0:OB1, :], b1.rearrange("e (j p) -> (e j) p", p=P)).then_inc(s_w["bias"], 16)
            sp.dma_start(bias_rows[OB1:BG, :], ob1.rearrange("(j p) -> j p", p=P)).then_inc(s_w["bias"], 16)
            sp.dma_start(bias_rows[BG:BG + DC, :], bg.rearrange("(j p) -> j p", p=P)).then_inc(s_w["bias"], 16)
            sp.dma_start(wo_raw, Wo.rearrange("(c p) d -> p c d", p=P)).then_inc(s_w["wo"], 16)
            load((0, 1))
            for dst, src in ((bo_b[:], bo), (ob2_b[:], ob2), (rb_b[:], router_b)):
                sp.dma_start(dst, src.partition_broadcast(P)).then_inc(s_w["bcast"], 16)
            sp.dma_start(rw_raw[:], router_w.rearrange("(c p) e -> p c e", p=P)).then_inc(s_w["rw"], 16)
            sp.dma_start(stage_w1(), ow1.rearrange("(c p) h -> p c h", p=P)).then_inc(s_w["ow"], 16)
            sp.dma_start(stage_w2(), ow2.rearrange("(c p) d -> p c d", p=P)).then_inc(s_w["ow"], 16)
            sp.dma_start(b2_b[:], b2.partition_broadcast(P)).then_inc(s_w["bcast"], 16)
            sp.wait_ge(s_const, 1)
            sp.dma_start(xbuf.rearrange("(n p) c -> p n c", p=P),
                         zrow[:].unsqueeze(1).to_broadcast([P, E * C // P, ROW])).then_inc(s_xbuf0, 16)

            def load_weights(e):
                i, v = e
                ei = i * 2 + v
                sp.dma_start(stage_w1(), w1[ei].rearrange("(c p) h -> p c h", p=P)).then_inc(s_we[0][v], 16)
                sp.dma_start(stage_w2(), w2[ei].rearrange("(c p) d -> p c d", p=P)).then_inc(s_we[1][v], 16)

            def store(g):
                i, v = g
                sp.wait_ge(s_out, cnt(g, 1, 1))
                sp.dma_start(out[i, v * GT:(v + 1) * GT, :].rearrange("(t p) d -> p t d", p=P), outt[v][:])\
                    .then_inc(s_st_out[v], 16)

            def step(i, u):
                prev, nxt, far = grp(i, u, -1), grp(i, u, 1), grp(i, u, 3)
                if live(prev, NG):
                    store(prev)
                if live(far, NG):
                    sp.wait_ge(s_x1, cnt(nxt, 1, 1))
                    load(far)

            step(-1, 1)
            sp.wait_ge(s_ow_hi, 4)
            sp.wait_ge(s_ow_lo, 4)
            load_weights((0, 0))
            for u in range(2):
                step(0, u)
            with sp.Fori(1, NG // 2 - 2) as i:
                for u in range(2):
                    step(i, u)
            for u in range(4):
                step(*grp(NG // 2 - 2, u, 0))
            def load_rows(e):
                i, v = e
                ei = i * 2 + v
                rows = xbuf.rearrange("(e c) w -> e c w", c=C)[ei]
                full = (C // P) * P
                sp.dma_start(xe[v][:, 0:C // P, 0:ROW], rows[0:full].rearrange("(t p) c -> p t c", p=P))\
                    .then_inc(s_xe[v], 16)
                sp.dma_start(xe[v][0:C - full, C // P, 0:ROW], rows[full:C]).then_inc(s_xe[v], 16)

            for v in range(2):
                sp.wait_ge(s_scat[v], landed((NG // 2 - 1, 0), TG))
            for v in range(2):
                load_rows((0, v))
            store((NG // 2 - 1, 1))
            sp.wait_ge(s_we_hi, 8)
            sp.wait_ge(s_we_lo, 8)
            load_weights((0, 1))

            def estep(i, u):
                prev, nxt, far = grp(i, u, -1), grp(i, u, 1), grp(i, u, 2)
                if live(prev, E):
                    sp.wait_ge(s_out, cnt(prev, 1, 1) + NG)
                    load_rows(nxt)
                sp.wait_ge(s_we_hi, cnt(nxt, 8, 8))
                sp.wait_ge(s_we_lo, cnt(nxt, 8, 8))
                load_weights(far)

            for u in range(2):
                estep(0, u)
            with sp.Fori(1, E // 2 - 1) as i:
                for u in range(2):
                    estep(i, u)
            sp.wait_ge(s_out, cnt((E // 2 - 2, 1), 1, 1) + NG)
            load_rows((E // 2 - 1, 1))

        @block.gpsimd
        def _(pool):
            pool.memset(ident[:], 0.0).then_inc(s_pc, 1)
            pool.memset(upto[:], 1.0).then_inc(s_pc, 1)
            pool.memset(ones[:], 1.0)
            pool.memset(mhalf[:], -0.5)
            pool.memset(zrow[:], 0.0).then_inc(s_pc, 1)
            pool.wait_ge(s_pc, 3)
            pool.affine_select(out=ident[:], in_=ident[:], compare_op=ALU.not_equal, fill=1.0, base=0,
                               pattern=[[-1, P]], channel_multiplier=1)
            pool.affine_select(out=upto[:], in_=upto[:], compare_op=ALU.is_ge, fill=0.0, base=0,
                               pattern=[[1, P]], channel_multiplier=-1)
            pool.memset(zrow[:, D:ROW], NOWHERE)
            pool.iota(first[:], pattern=[[-1, E]], base=E, channel_multiplier=0, allow_small_or_imprecise_dtypes=True)
            pool.iota(row0[:], pattern=[[C, E]], base=-1, channel_multiplier=0, allow_small_or_imprecise_dtypes=True)
            pool.iota(id_int[:], pattern=[[GT, 2], [P, TG]], base=0, channel_multiplier=1).then_inc(s_const, 1)
            pool.wait_ge(s_const, 1)
            for v in range(2):
                pool.tensor_copy(x1[v][:, :, D:ROW], id_int[:, v, :].unsqueeze(2)).then_inc(s_id, 1)

            def deviation(k, g, n, extra=0):
                pool.wait_ge(s_ve[k], cnt(g, 1, 1) + extra)
                pool.tensor_tensor(rstd[k][:, 0:n], veps[k][:, 0:n], mhalf[:, 0:n], ALU.pow).then_inc(s_rs[k], 1)
                pool.wait_ge(s_rs[k], cnt(g, 1, 1) + extra)
                pool.tensor_tensor(nmr[k][:, 0:n], nmean[k][:, 0:n], rstd[k][:, 0:n], ALU.mult).then_inc(s_nm[k], 1)

            def norm0(g):
                i, v = g
                deviation(0, g, TG)
                pool.wait_ge(s_nm[0], cnt(g, 1, 1))
                pool.wait_ge(s_T0, cnt(g, 2, 0))
                pool.sem_inc(s_held, 1)
                for t in range(TG):
                    last = pool.tensor_scalar(tok[:, t, :], xin[v][:, t, :], rstd[0][:, t:t + 1], nmr[0][:, t:t + 1],
                                              ALU.mult, ALU.add)
                last.then_inc(s_tok, 1)

            def dispatch(g, tiles):
                i, v = g
                pool.wait_ge(s_idx, cnt(g, 1, 1))
                pool.sem_inc(s_held, 1)
                for t in tiles:
                    pool.indirect_dma_start(out=xbuf, out_offset=bass.IndirectOffsetOnAxis(idx[v][:, t:t + 1], 0),
                                            in_=x1[v][:, t, 0:ROW], in_offset=None, bounds_check=E * C - 1,
                                            oob_is_err=False).then_inc(s_scat[v], 16)

            def renumber(g):
                i, v = g
                if live(grp(i, v, -2), NG):
                    pool.wait_ge(s_scat[v], landed(grp(i, v, -2), TG))
                    pool.sem_inc(s_held, 1)
                    pool.tensor_scalar(x1[v][:, :, D:ROW], x1[v][:, :, D:ROW], float(2 * GT), None, ALU.add)\
                        .then_inc(s_id, 1)

            def norm2(g, src, n, base=0):
                i, v = g
                deviation(2, g, n, base)
                pool.wait_ge(s_nm[2], cnt(g, 1, 1) + base)
                pool.wait_ge(s_T1, cnt(g, 2, 0) + 2 * base)
                pool.sem_inc(s_held, 1)
                for t in range(n):
                    last = pool.tensor_scalar(tok2[:, t, :], src[v][:, t, 0:D], rstd[2][:, t:t + 1],
                                              nmr[2][:, t:t + 1], ALU.mult, ALU.add)
                last.then_inc(s_tok2, 1)

            def state_lo(g):
                i, v = g
                pool.wait_ge(s_wo, cnt(g, 2, 0))
                for c in range(DC):
                    pool.wait_ge(s_h_hi, cnt(g, 2, c + 1))
                    pool.tensor_tensor(hst_lo[:, c, :], hst[v][:, c, :], hst_hi[:, c, :].bitcast(F32), ALU.subtract)\
                        .then_inc(s_h_lo, 1)

            def step(i, u):
                prev, now, nxt, far = grp(i, u, -1), grp(i, u, 0), grp(i, u, 1), grp(i, u, 2)
                if live(prev, NG):
                    deviation(3, prev, TG)
                if live(far, NG):
                    norm0(far)
                if live(prev, NG):
                    residual2(prev)
                if live(nxt, NG):
                    deviation(1, nxt, TG)
                    renumber(nxt)
                if live(now, NG):
                    dispatch(now, range(TG))
                if live(nxt, NG):
                    norm2(nxt, x1, TG)
                if live(far, NG):
                    state_lo(far)

            def residual2(g):
                i, v = g
                pool.wait_ge(s_z, cnt(g, 1, 1))
                if live(grp(i, v, -2), NG):
                    pool.wait_ge(s_st_out[v], landed(grp(i, v, -2)))
                pool.tensor_tensor(outt[v][:], ysb[:], x1[v][:, :, 0:D], ALU.add).then_inc(s_out, 1)

            step(-1, 0)
            step(-1, 1)
            pool.wait_ge(s_xbuf0, 16)
            for u in range(2):
                step(0, u)
            with pool.Fori(1, NG // 2 - 1) as i:
                for u in range(2):
                    step(i, u)
            for u in range(2):
                step(NG // 2 - 1, u)

            def enorm(e):
                i, v = e
                norm2(e, xe, ET, NG)
                if live(grp(i, v, -2), E):
                    pool.wait_ge(s_fin[v], landed(grp(i, v, -2), ET))
                pool.sem_inc(s_held, 1)
                pool.tensor_copy(oidx[v][:].unsqueeze(2), xe[v][:, 0:ET, D:ROW]).then_inc(s_oidx, 1)

            def finish(e):
                i, v = e
                deviation(3, e, ET, NG)
                pool.wait_ge(s_z, cnt(e, 1, 1) + NG)
                pool.tensor_tensor(outt[v][:, 0:ET, :], ysb[:, 0:ET, :], xe[v][:, 0:ET, 0:D], ALU.add)\
                    .then_inc(s_out, 1)
                pool.wait_ge(s_out, cnt(e, 1, 1) + NG)
                pool.wait_ge(s_oidx, cnt(e, 1, 1))
                pool.sem_inc(s_held, 1)
                for t in range(ET):
                    n = min(P, C - t * P)
                    pool.indirect_dma_start(out=out_rows, out_offset=bass.IndirectOffsetOnAxis(oidx[v][0:n, t:t + 1], 0),
                                            in_=outt[v][0:n, t, :], in_offset=None, bounds_check=N - 1,
                                            oob_is_err=False).then_inc(s_fin[v], 16)

            def estep(i, u):
                now, nxt = grp(i, u, 0), grp(i, u, 1)
                if live(nxt, E):
                    enorm(nxt)
                finish(now)

            enorm((0, 0))
            deviation(3, (NG // 2 - 1, 1), TG)
            residual2((NG // 2 - 1, 1))
            for v in range(2):
                pool.wait_ge(s_st_out[v], landed((NG // 2 - 1, 0)))
            for u in range(2):
                estep(0, u)
            with pool.Fori(1, E // 2 - 1) as i:
                for u in range(2):
                    estep(i, u)
            for u in range(2):
                estep(E // 2 - 1, u)
            for v in range(2):
                pool.wait_ge(s_fin[v], landed((E // 2 - 1, 0), ET))

        @block.scalar
        def _(act):
            act.wait_ge(s_w["bias"], 48)
            act.wait_ge(s_wT, 1)
            act.activation(biasT[:], psT[:, 0, 0:P], ACT.Copy).then_inc(s_biasT, 1)
            for n, W in enumerate((WgT, WoT)):
                act.wait_ge(s_wT, n + 2)
                act.activation(W[0][:], psA_t[:, 2 * n:2 * n + 2, :], ACT.Copy).then_inc(s_wT_hi, 1)

            def relu(g, j, n, bias, base=0):
                act.wait_ge(s_l1, cnt(g, HC, j + 1) + base)
                act.wait_ge(s_hid_lo, cnt(g, HC, max(j - 1, 0)) + base)
                act.activation(hid[j % 2][:, 0:n], psH[:, j % 2, 0:n], ACT.Relu, bias=bias).then_inc(s_hid, 1)
                act.wait_ge(s_hid, cnt(g, HC, j + 1) + base)
                act.wait_ge(s_l2, cnt(g, HC, max(j - 3, 0)) + base)
                act.activation(hid_hi[j % 4][:, 0:n], hid[j % 2][:, 0:n], ACT.Copy).then_inc(s_hid_hi, 1)

            def norm1(g):
                act.wait_ge(s_nm[1], cnt(g, 1, 1))
                act.wait_ge(s_att, cnt(g, 2, 2))
                for t in range(TG):
                    last = act.activation(att[:, t, :], att[:, t, :], ACT.Identity, bias=nmr[1][:, t:t + 1],
                                          scale=rstd[1][:, t:t + 1])
                last.then_inc(s_u, 1)

            def norm3(g, n, base=0):
                act.wait_ge(s_nm[3], cnt(g, 1, 1) + base)
                act.wait_ge(s_y, cnt(g, 2, 2) + 2 * base)
                for t in range(n):
                    last = act.activation(ysb[:, t, :], ysb[:, t, :], ACT.Identity, bias=nmr[3][:, t:t + 1],
                                          scale=rstd[3][:, t:t + 1])
                last.then_inc(s_z, 1)

            def xn_hi(g):
                act.wait_ge(s_gate, cnt(g, 2, 0))
                act.wait_ge(s_scan, cnt(g, 2, 0))
                for c in range(DC):
                    act.wait_ge(s_T0, cnt(g, 2, c + 1))
                    act.activation(xnT[:, c, :], psT[:, c, :], ACT.Copy)
                    act.activation(xnT_hi[:, c, :], psT[:, c, :], ACT.Copy).then_inc(s_xn_hi, 1)

            def sigmoid(g):
                act.wait_ge(s_scan, cnt(g, 2, 0))
                for c in range(DC):
                    act.wait_ge(s_gate, cnt(g, 2, c + 1))
                    act.activation(keep[:, c, :], psA[:, c, :], ACT.Sigmoid, bias=neg_bg[:, c:c + 1], scale=-1.0)\
                        .then_inc(s_keep, 1)

            def state_hi(g):
                i, v = g
                act.wait_ge(s_wo, cnt(g, 2, 0))
                for c in range(DC):
                    act.wait_ge(s_scan, cnt(g, 2, c + 1))
                    act.activation(hst_hi[:, c, :], hst[v][:, c, :], ACT.Copy).then_inc(s_h_hi, 1)

            def xf_hi(g, n, base=0):
                act.wait_ge(s_l1, cnt(g, HC, 0) + HC * base)
                act.wait_ge(s_lg, cnt(g, 1, 0) if not base else NG)
                for c in range(DC):
                    act.wait_ge(s_T1, cnt(g, 2, c + 1) + 2 * base)
                    act.activation(xfT_hi[:, c, 0:n], psT[:, c, 0:n], ACT.Copy).then_inc(s_xf_hi, 1)

            def weights_hi(e, j):
                i, v = e
                m, q = j // 4, j % 4
                if q == 0:
                    act.wait_ge(s_we[m][v], landed(e))
                dst = (W1, W2)[m][v][0][:].rearrange("p a b -> p (a b)")
                act.activation(dst[:, q * 512:(q + 1) * 512], stage[:, m, q * 512:(q + 1) * 512], ACT.Copy)\
                    .then_inc(s_we_hi, 1)

            def step(i, u):
                now, nxt, far = grp(i, u, 0), grp(i, u, 1), grp(i, u, 2)
                run, up, ahead = live(now, NG), live(nxt, NG), live(far, NG)

                def hidden(js):
                    if run:
                        for j in js:
                            relu(now, j, GT, biasT[:, OB1 + j:OB1 + j + 1])

                hidden(range(0, 2))
                if live(grp(i, u, -1), NG):
                    norm3(grp(i, u, -1), TG)
                hidden(range(2, 4))
                if ahead:
                    xn_hi(far)
                hidden(range(4, 5))
                if up:
                    norm1(nxt)
                if not ahead:
                    for j in range(4 * u, 4 * u + 4):
                        weights_hi((0, 0), j)
                hidden(range(5, 6))
                if ahead:
                    sigmoid(far)
                hidden(range(6, 8))
                if up:
                    xf_hi(nxt, GT)
                if ahead:
                    state_hi(far)

            act.wait_ge(s_biasT, 2)
            step(-1, 0)
            act.wait_ge(s_w["rw"], 16)
            act.activation(rw[:, :, 0:E], rw_raw[:], ACT.Copy).then_inc(s_rw_hi, 1)
            act.wait_ge(s_w["ow"], 32)
            for m, W in enumerate((W1, W2)):
                for q in range(2):
                    dst = W[1][0][:].rearrange("p a b -> p (a b)")
                    act.activation(dst[:, q * 1024:(q + 1) * 1024], stage[:, m, q * 1024:(q + 1) * 1024], ACT.Copy)\
                        .then_inc(s_ow_hi, 1)
            step(-1, 1)
            for u in range(2):
                step(0, u)
            with act.Fori(1, NG // 2 - 1) as i:
                for u in range(2):
                    step(i, u)
            for u in range(2):
                step(NG // 2 - 1, u)

            def estep(i, u):
                prev, now, nxt = grp(i, u, -1), grp(i, u, 0), grp(i, u, 1)
                more = live(nxt, E)
                for j in range(HC):
                    col = (now[0] * 2 + now[1]) * HC + j
                    relu(now, j, C, biasT[:, bass.ds(col, 1)], EL1)
                    if j == 0:
                        if live(prev, E):
                            norm3(prev, ET, NG)
                        else:
                            norm3((NG // 2 - 1, 1), TG)
                    if more:
                        if j == 0:
                            act.wait_ge(s_l2, cnt(now, HC, 0) + EL1)
                        weights_hi(nxt, j)
                if more:
                    xf_hi(nxt, C, NG)

            xf_hi((0, 0), C, NG)
            for u in range(2):
                estep(0, u)
            with act.Fori(1, E // 2 - 1) as i:
                for u in range(2):
                    estep(i, u)
            for u in range(2):
                estep(E // 2 - 1, u)
            norm3((E // 2 - 1, 1), ET, NG)

        @block.vector
        def _(dve):
            dve.memset(bias_rows[:], 0.0).then_inc(s_bias_z, 1)
            dve.memset(seen[:], 0.0).then_inc(s_seen, 1)
            dve.wait_ge(s_biasT, 1)
            dve.tensor_scalar(neg_bg[:], biasT[:, BG:BG + DC], -1.0, None, ALU.mult).then_inc(s_biasT, 1)
            for n, W in enumerate((WgT, WoT)):
                dve.wait_ge(s_wT_hi, n + 1)
                dve.tensor_tensor(W[1][:], psA_t[:, 2 * n:2 * n + 2, :], W[0][:].bitcast(F32), ALU.subtract)\
                    .then_inc(s_wT_lo, 1)

            def stats(k, src, g, n, base=0):
                for t in range(n):
                    last = dve.bn_stats(st[k][:, t, :], src(t))
                last.then_inc(s_st[k], 1)
                dve.wait_ge(s_st[k], cnt(g, 1, 1) + base)
                dve.sem_inc(s_held_v, 1)
                for t in range(n):
                    last = dve.bn_aggr(mv[k][:, t, :], st[k][:, t, :])
                last.then_inc(s_ag[k], 1)
                dve.wait_ge(s_nm[k], cnt(g, 1, 0) + base)
                dve.wait_ge(s_ag[k], cnt(g, 1, 1) + base)
                dve.tensor_scalar(veps[k][:, 0:n].unsqueeze(2), mv[k][:, 0:n, 1:2], EPS, None, ALU.add)
                dve.tensor_scalar(nmean[k][:, 0:n].unsqueeze(2), mv[k][:, 0:n, 0:1], -1.0, None, ALU.mult)\
                    .then_inc(s_ve[k], 1)

            def stats0(g):
                i, v = g
                dve.wait_ge(s_x_in[v], landed(g))
                stats(0, lambda t: xin[v][:, t, :], g, TG)

            def xn_lo(g):
                dve.wait_ge(s_gate, cnt(g, 2, 0))
                for c in range(DC):
                    dve.wait_ge(s_xn_hi, cnt(g, 2, c + 1))
                    dve.tensor_tensor(xnT_lo[:, c, :], xnT[:, c, :], xnT_hi[:, c, :].bitcast(F32), ALU.subtract)\
                        .then_inc(s_xn_lo, 1)

            def recurrence(g):
                i, v = g
                if live(grp(i, v, -2), NG):
                    dve.wait_ge(s_h_lo, cnt(grp(i, v, -2), 2, 2))
                for c in range(DC):
                    dve.wait_ge(s_keep, cnt(g, 2, c + 1))
                    dve.scalar_tensor_tensor(out=xnT[:, c, :], in0=keep[:, c, :], scalar=-1.0, in1=xnT[:, c, :],
                                             op0=ALU.add, op1=ALU.mult).then_inc(s_ngx, 1)
                    if v == 1:
                        dve.wait_ge(s_scan, cnt(g, 2, 0))
                    dve.wait_ge(s_ngx, cnt(g, 2, c + 1))
                    carry = hst[0][:, c, GT - 1:GT] if v == 1 else 0.0
                    dve.tensor_tensor_scan(hst[v][:, c, :], keep[:, c, :], xnT[:, c, :], carry, ALU.mult,
                                           ALU.subtract).then_inc(s_scan, 1)

            def attended(g):
                for a in range(2):
                    dve.wait_ge(s_wo, cnt(g, 2, a + 1))
                    dve.tensor_tensor(att[:, 2 * a:2 * a + 2, :], psA_t[:, 2 * a:2 * a + 2, :],
                                      bo_b[:].unsqueeze(1).to_broadcast([P, 2, D]), ALU.add).then_inc(s_att, 1)

            def stats1(g):
                dve.wait_ge(s_att, cnt(g, 2, 2))
                stats(1, lambda t: att[:, t, :], g, TG)

            def residual1(g):
                i, v = g
                if live(grp(i, v, -2), NG):
                    dve.wait_ge(s_scat[v], landed(grp(i, v, -2), TG))
                    dve.wait_ge(s_out, cnt(grp(i, v, -2), 1, 1))
                dve.wait_ge(s_u, cnt(g, 1, 1))
                dve.tensor_tensor(x1[v][:, :, 0:D], att[:], xin[v][:], ALU.add).then_inc(s_x1, 1)

            def stats2(g):
                dve.wait_ge(s_x1, cnt(g, 1, 1))
                stats(2, lambda t: x1[g[1]][:, t, 0:D], g, TG)

            def xf_lo(g, n, base=0):
                for c in range(DC):
                    dve.wait_ge(s_xf_hi, cnt(g, 2, c + 1) + 2 * base)
                    dve.tensor_tensor(xfT_lo[:, c, 0:n], psT[:, c, 0:n], xfT_hi[:, c, 0:n].bitcast(F32),
                                      ALU.subtract).then_inc(s_xf_lo, 1)

            def choose(g):
                def link(n):
                    dve.wait_ge(s_rt, cnt(g, 6, n))

                dve.wait_ge(s_lg, cnt(g, 1, 1))
                dve.tensor_tensor(lg[0][:], logits[:, :, 0:E], rb_b[:].unsqueeze(1).to_broadcast([P, TG, E]), ALU.add)\
                    .then_inc(s_rt, 1)
                link(1)
                dve.tensor_tensor(lg[1][:], logits[:, :, E:2 * E], lg[0][:], ALU.add).then_inc(s_rt, 1)
                link(2)
                dve.tensor_reduce(lmax[:], lg[1][:], AX_X, ALU.max).then_inc(s_rt, 1)
                link(3)
                dve.tensor_tensor(lg[2][:], lg[1][:], lmax[:].unsqueeze(2).to_broadcast([P, TG, E]), ALU.subtract)\
                    .then_inc(s_rt, 1)
                link(4)
                dve.scalar_tensor_tensor(out=cand[:], in0=lg[2][:], scalar=-TIE,
                                         in1=first[:].unsqueeze(1).to_broadcast([P, TG, E]), op0=ALU.is_ge,
                                         op1=ALU.mult).then_inc(s_rt, 1)
                link(5)
                dve.tensor_reduce(cmax[:], cand[:], AX_X, ALU.max).then_inc(s_rt, 1)
                link(6)
                if live(grp(g[0], g[1], -1), NG):
                    dve.wait_ge(s_rank, cnt(g, 1, 0))
                dve.tensor_tensor(oh[:], cand[:], cmax[:].unsqueeze(2).to_broadcast([P, TG, E]), ALU.is_equal)\
                    .then_inc(s_oh, 1)

            def place(g):
                i, v = g

                def link(n):
                    dve.wait_ge(s_sl, cnt(g, 4, n))

                dve.wait_ge(s_rank, cnt(g, 1, 1))
                dve.tensor_tensor(rk[0][:], ranks, row0[:].unsqueeze(1).to_broadcast([P, TG, E]), ALU.add)
                dve.tensor_scalar(rk[1][:], ranks, C + 0.5, NOWHERE, ALU.is_ge, ALU.mult)
                dve.tensor_reduce(seen_g[:], oh[:].rearrange("p t e -> p e t"), AX_X, ALU.add).then_inc(s_sl, 1)
                link(1)
                dve.tensor_tensor(rk[2][:], rk[0][:], rk[1][:], ALU.add).then_inc(s_sl, 1)
                dve.tensor_tensor(seen[:], seen[:], seen_g[:], ALU.add).then_inc(s_seen, 1)
                link(2)
                dve.tensor_tensor(rk[3][:], rk[2][:], oh[:], ALU.mult).then_inc(s_sl, 1)
                link(3)
                dve.tensor_reduce(slot[:], rk[3][:], AX_X, ALU.add).then_inc(s_sl, 1)
                link(4)
                if live(grp(i, v, -2), NG):
                    dve.wait_ge(s_scat[v], landed(grp(i, v, -2), TG))
                dve.tensor_copy(idx[v][:], slot[:]).then_inc(s_idx, 1)

            def lo(g, j, n, base=0):
                dve.wait_ge(s_hid_hi, cnt(g, HC, j + 1) + base)
                dve.tensor_tensor(hid_lo[j % 4][:, 0:n], hid[j % 2][:, 0:n], hid_hi[j % 4][:, 0:n].bitcast(F32),
                                  ALU.subtract).then_inc(s_hid_lo, 1)

            def result(g, bias, n, base=0):
                dve.wait_ge(s_l2, cnt(g, HC, HC) + HC * base)
                if base or live(grp(g[0], g[1], -1), NG):
                    dve.wait_ge(s_out, cnt(g, 1, 0) + base)
                for a in range(2):
                    k = min(n - 2 * a, 2)
                    dve.tensor_tensor(ysb[:, 2 * a:2 * a + k, :], psY_t[:, 2 * a:2 * a + k, :],
                                      bias.to_broadcast([P, k, D]), ALU.add).then_inc(s_y, 1)

            def stats3(g, n, base=0):
                dve.wait_ge(s_y, cnt(g, 2, 2) + 2 * base)
                stats(3, lambda t: ysb[:, t, :], g, n, base)

            def weights_lo(e, j):
                i, v = e
                m, q = j // 4, j % 4
                hi = (W1, W2)[m][v][0][:].rearrange("p a b -> p (a b)")[:, q * 512:(q + 1) * 512]
                dst = (W1, W2)[m][v][1][:].rearrange("p a b -> p (a b)")[:, q * 512:(q + 1) * 512]
                dve.wait_ge(s_we_hi, cnt(e, 8, j + 1))
                dve.tensor_tensor(dst, stage[:, m, q * 512:(q + 1) * 512], hi.bitcast(F32), ALU.subtract)\
                    .then_inc(s_we_lo, 1)

            def estats(e):
                i, v = e
                dve.wait_ge(s_xe[v], landed(e, 2))
                stats(2, lambda t: xe[v][:, t, 0:D], e, ET, NG)

            def step(i, u):
                now, nxt, far = grp(i, u, 0), grp(i, u, 1), grp(i, u, 2)
                run, up, ahead = live(now, NG), live(nxt, NG), live(far, NG)

                def low(*js):
                    if run:
                        for j in js:
                            lo(now, j, GT)

                low(0)
                if ahead:
                    stats0(far)
                if run:
                    place(now)
                low(1)
                if up:
                    attended(nxt)
                low(2)
                if up:
                    stats1(nxt)
                low(3)
                if ahead:
                    xn_lo(far)
                low(4)
                if up:
                    residual1(nxt)
                    stats2(nxt)
                low(5)
                if ahead:
                    recurrence(far)
                else:
                    for j in range(4 * u, 4 * u + 4):
                        weights_lo((0, 0), j)
                low(6)
                if run and not up:
                    estats((0, 0))
                low(7)
                if up:
                    xf_lo(nxt, GT)
                elif run:
                    xf_lo((0, 0), C, NG)
                if run:
                    result(now, ob2_b[:].unsqueeze(1), TG)
                if up:
                    choose(nxt)
                if run:
                    stats3(now, TG)

            step(-1, 0)
            dve.wait_ge(s_rw_hi, 1)
            dve.tensor_tensor(rw[:, :, E:2 * E], rw_raw[:], rw[:, :, 0:E].bitcast(F32), ALU.subtract).then_inc(s_rw_lo, 1)
            for m, W in enumerate((W1, W2)):
                for q in range(2):
                    hi = W[1][0][:].rearrange("p a b -> p (a b)")[:, q * 1024:(q + 1) * 1024]
                    dst = W[1][1][:].rearrange("p a b -> p (a b)")[:, q * 1024:(q + 1) * 1024]
                    dve.wait_ge(s_ow_hi, 2 * m + q + 1)
                    dve.tensor_tensor(dst, stage[:, m, q * 1024:(q + 1) * 1024], hi.bitcast(F32), ALU.subtract)\
                        .then_inc(s_ow_lo, 1)
            dve.wait_ge(s_w["bcast"], 64)
            step(-1, 1)

            for u in range(2):
                step(0, u)
            with dve.Fori(1, NG // 2 - 1) as i:
                for u in range(2):
                    step(i, u)
            for u in range(2):
                step(NG // 2 - 1, u)

            def estep(i, u):
                now, nxt = grp(i, u, 0), grp(i, u, 1)
                for j in range(HC):
                    lo(now, j, C, EL1)
                    if live(nxt, E):
                        weights_lo(nxt, j)
                        if j == 4:
                            estats(nxt)
                if live(nxt, E):
                    xf_lo(nxt, C, NG)
                ei = now[0] * 2 + now[1]
                result(now, b2_b[:, bass.ds(ei, 1), :], ET, NG)
                stats3(now, ET, NG)

            for u in range(2):
                estep(0, u)
            with dve.Fori(1, E // 2 - 1) as i:
                for u in range(2):
                    estep(i, u)
            for u in range(2):
                estep(E // 2 - 1, u)

        @block.tensor
        def _(pe):
            def blocks(dst, src, t, c, inc=None):
                mm = pe.transpose(dst, src, ident[:])
                return mm

            pe.wait_ge(s_const, 1)
            pe.wait_ge(s_w["bias"], 48)
            pe.transpose(psT[:, 0, 0:P], bias_rows[:], ident[:]).then_inc(s_wT, 1)
            for n, (name, raw) in enumerate((("wg", outt[0]), ("wo", outt[1]))):
                pe.wait_ge(s_w[name], 16)
                for c in range(DC):
                    for a in range(DC):
                        last = pe.transpose(psA_t[:, 2 * n + c, a * P:(a + 1) * P], raw[:, a, c * P:(c + 1) * P],
                                            ident[:])
                last.then_inc(s_wT, 1)

            def split_product(dst, w, ws, r, rs, k, last_k):
                w_hi, w_lo = w[0][ws], w[1][ws]
                r_hi, r_lo = r[0][rs], r[1][rs]
                pe.matmul(dst, w_hi, r_hi, start=(k == 0), stop=False)
                pe.matmul(dst, w_hi, r_lo, start=False, stop=False)
                return pe.matmul(dst, w_lo, r_hi, start=False, stop=(k == last_k))

            ALL = slice(None)

            def transposes0(g):
                pe.wait_ge(s_tok, cnt(g, 1, 1))
                prev = grp(g[0], g[1], -2)
                if live(prev, NG):
                    pe.wait_ge(s_idx, cnt(prev, 1, 1))
                for c in range(DC):
                    for t in range(TG):
                        last = pe.transpose(psT[:, c, t * P:(t + 1) * P], tok[:, t, c * P:(c + 1) * P], ident[:])
                    last.then_inc(s_T0, 1)

            def gate(g):
                pe.wait_ge(s_xn_hi, cnt(g, 2, 2))
                pe.wait_ge(s_xn_lo, cnt(g, 2, 2))
                prev = grp(g[0], g[1], -1)
                if live(prev, NG):
                    pe.wait_ge(s_att, cnt(prev, 2, 2))
                for m in range(DC):
                    for k in range(DC):
                        last = split_product(psA[:, m, :], WgT, (ALL, k, slice(m * P, (m + 1) * P)),
                                             (xnT_hi, xnT_lo), (ALL, k, ALL), k, DC - 1)
                    last.then_inc(s_gate, 1)

            def project(g):
                pe.wait_ge(s_keep, cnt(g, 2, 2))
                pe.wait_ge(s_h_hi, cnt(g, 2, 2))
                pe.wait_ge(s_h_lo, cnt(g, 2, 2))
                for t in range(TG):
                    for k in range(DC):
                        last = split_product(psA_t[:, t, :], (hst_hi, hst_lo), (ALL, k, slice(t * P, (t + 1) * P)),
                                             WoT, (ALL, k, ALL), k, DC - 1)
                    if t % 2:
                        last.then_inc(s_wo, 1)

            def transposes1(g, n, base=0):
                pe.wait_ge(s_tok2, cnt(g, 1, 1) + base)
                if base == 0:
                    far = grp(g[0], g[1], 1)
                    if live(far, NG):
                        pe.wait_ge(s_xn_hi, cnt(far, 2, 2))
                    elif live(g, NG):
                        pe.wait_ge(s_idx, cnt(g, 1, 0))
                else:
                    pe.wait_ge(s_xf_lo, cnt(g, 2, 0) + 2 * base)
                    pe.wait_ge(s_xf_hi, cnt(g, 2, 0) + 2 * base)
                    pe.wait_ge(s_idx, NG)
                for c in range(DC):
                    for t in range(n):
                        last = pe.transpose(psT[:, c, t * P:(t + 1) * P], tok2[:, t, c * P:(c + 1) * P], ident[:])
                    last.then_inc(s_T1, 1)

            def route(g):
                pe.wait_ge(s_xf_hi, cnt(g, 2, 2))
                pe.wait_ge(s_xf_lo, cnt(g, 2, 2))
                for t in range(TG):
                    for k in range(DC):
                        pe.matmul(logits[:, t, :], xfT_hi[:, k, t * P:(t + 1) * P], rw[:, k, :], start=(k == 0),
                                  stop=False)
                        last = pe.matmul(logits[:, t, 0:E], xfT_lo[:, k, t * P:(t + 1) * P], rw[:, k, 0:E],
                                         start=False, stop=(k == DC - 1))
                last.then_inc(s_lg, 1)

            def rank(g):
                pe.wait_ge(s_seen, cnt(g, 1, 1))
                pe.wait_ge(s_oh, cnt(g, 1, 1))
                pe.matmul(ranks, upto[:], oh[:], start=True, stop=False)
                pe.matmul(ranks, ones[:], seen[:].unsqueeze(1).to_broadcast([P, TG, E]), start=False, stop=False)
                for k in range(1, TG):
                    last = pe.matmul(ranks[:, k:TG, :], ones[:], oh[:, 0:TG - k, :], start=False, stop=(k == TG - 1))
                last.then_inc(s_rank, 1)

            def layer1(g, j, n, w, base=0):
                pe.wait_ge(s_hid, cnt(g, HC, max(j - 1, 0)) + base)
                for k in range(DC):
                    last = split_product(psH[:, j % 2, 0:n], w, (ALL, k, slice(j * P, (j + 1) * P)),
                                         (xfT_hi, xfT_lo), (ALL, k, slice(0, n)), k, DC - 1)
                last.then_inc(s_l1, 1)

            def layer2(g, j, n, w, base=0):
                pe.wait_ge(s_hid_lo, cnt(g, HC, j + 1) + base)
                for t in range(n):
                    tile = (ALL, slice(t * P, (t + 1) * P))
                    hi, lo_ = hid_hi[j % 4][tile], hid_lo[j % 4][tile]
                    pe.matmul(psY_t[:, t, :], hi, w[0][:, j, :], start=(j == 0 and t % 2 == 0), stop=False,
                              skip_group_check=True)
                    pe.matmul(psY_t[:, t, :], hi, w[1][:, j, :], start=False, stop=False, skip_group_check=True)
                    last = pe.matmul(psY_t[:, t, :], lo_, w[0][:, j, :], start=False, stop=(j == HC - 1),
                                     skip_group_check=True)
                last.then_inc(s_l2, 1)

            def step(i, u):
                now, nxt, far = grp(i, u, 0), grp(i, u, 1), grp(i, u, 2)
                run, up, ahead = live(now, NG), live(nxt, NG), live(far, NG)
                if run:
                    layer1(now, 0, GT, W1[1])
                    layer1(now, 1, GT, W1[1])
                    rank(now)
                if up:
                    project(nxt)
                for j in range(2, HC):
                    if run:
                        layer1(now, j, GT, W1[1])
                        if j == 2 and live(grp(i, u, -1), NG):
                            pe.wait_ge(s_y, cnt(now, 2, 0))
                        layer2(now, j - 2, TG, W2[1])
                    if j == 3 and ahead:
                        transposes0(far)
                    if j == 5 and ahead:
                        gate(far)
                if up:
                    transposes1(nxt, TG)
                elif run:
                    transposes1((0, 0), ET, NG)
                if run:
                    layer2(now, HC - 2, TG, W2[1])
                    layer2(now, HC - 1, TG, W2[1])
                if up:
                    route(nxt)

            pe.wait_ge(s_wT_lo, 2)
            step(-1, 0)
            pe.wait_ge(s_rw_lo, 1)
            step(-1, 1)
            pe.wait_ge(s_ow_lo, 4)
            for u in range(2):
                step(0, u)
            with pe.Fori(1, NG // 2 - 1) as i:
                for u in range(2):
                    step(i, u)
            for u in range(2):
                step(NG // 2 - 1, u)

            def estep(i, u):
                now, nxt = grp(i, u, 0), grp(i, u, 1)
                pe.wait_ge(s_we_lo, cnt(now, 8, 4))
                pe.wait_ge(s_xf_hi, cnt(now, 2, 2) + 2 * NG)
                pe.wait_ge(s_xf_lo, cnt(now, 2, 2) + 2 * NG)
                for j in range(HC + 2):
                    if j < HC:
                        layer1(now, j, C, W1[u], EL1)
                    if j == HC and live(nxt, E):
                        transposes1(nxt, ET, NG)
                    if j >= 2:
                        if j == 2:
                            pe.wait_ge(s_y, cnt(now, 2, 0) + 2 * NG)
                            pe.wait_ge(s_we_lo, cnt(now, 8, 8))
                        layer2(now, j - 2, ET, W2[u], EL1)

            for u in range(2):
                estep(0, u)
            with pe.Fori(1, E // 2 - 1) as i:
                for u in range(2):
                    estep(i, u)
            for u in range(2):
                estep(E // 2 - 1, u)


_INS = ["L0_attn_x", "L0_attn_Wg", "L0_attn_bg", "L0_attn_Wo", "L0_attn_bo", "L0_ffn_router_w", "L0_ffn_router_b",
        "L0_ffn_w1", "L0_ffn_b1", "L0_ffn_w2", "L0_ffn_b2", "L0_ffn_ow1", "L0_ffn_ob1", "L0_ffn_ow2", "L0_ffn_ob2"]


def kernel(**inputs):
    import numpy as np
    import concourse.bacc as bacc
    from concourse.bass_utils import run_bass_kernel_spmd

    nc = bacc.Bacc("TRN2", target_bir_lowering=False, num_devices=1)
    arrays, args = {}, []
    for name in _INS:
        a = np.ascontiguousarray(inputs[name])
        arrays[name] = a
        args.append(nc.dram_tensor(name, a.shape, mybir.dt.from_np(a.dtype), kind="ExternalInput").ap())
    args.append(nc.dram_tensor("out", arrays["L0_attn_x"].shape, F32, kind="ExternalOutput").ap())
    sandwich_kernel(nc, *args)
    r = run_bass_kernel_spmd(nc, [arrays], core_ids=[0])
    return r.results[0]["out"]
```

```python
from contextlib import ExitStack

import concourse.bass as bass
from concourse import mybir

ALU = mybir.AluOpType
ACT = mybir.ActivationFunctionType
F32 = mybir.dt.float32
F32R = mybir.dt.float32r
BF16 = mybir.dt.bfloat16
I32 = mybir.dt.int32
AX_X = mybir.AxisListType.X

P = 128
D = 256
DC = D // P
H = 1024
HC = H // P
E = 8
C = 320
TG = 4
GT = TG * P
ROW = D + 1
PITCH = 260
ET = -(-C // P)
EPS = 1e-5
NOWHERE = 1.0e6
TIE = 2.0 ** -25


def grp(i, u, k):
    return i + (u + k) // 2, (u + k) % 2


def cnt(g, n, k):
    return g[0] * (2 * n) + (g[1] * n + k)


def landed(g, n=1):
    return g[0] * (16 * n) + 16 * n


def live(g, n):
    return not isinstance(g[0], int) or 0 <= 2 * g[0] + g[1] < n


def sandwich_kernel(nc, x, Wg, bg, Wo, bo, router_w, router_b, w1, b1, w2, b2, ow1, ob1, ow2, ob2, out):
    B, L, _ = x.shape
    N = B * L
    NG = N // GT
    assert L == 2 * GT and Wg.shape == (D, D) and w1.shape == (E, D, H)
    out_rows = out.rearrange("b l d -> (b l) d")

    with ExitStack() as ctx:
        def sb(name, shape, dt=F32):
            return ctx.enter_context(nc.sbuf_tensor(name, shape, dt))

        def sem(name):
            return ctx.enter_context(nc.semaphore(name))

        def sems(name):
            return [sem(f"{name}{v}") for v in range(2)]

        xbuf = nc.dram_tensor("xbuf", [E * C, ROW], F32).ap()

        stage = sb("stage", [P, 2, 2048])
        WgT = [sb(f"WgT_{p}", [P, DC, D], F32R) for p in ("hi", "lo")]
        WoT = [sb(f"WoT_{p}", [P, DC, D], F32R) for p in ("hi", "lo")]
        rw = sb("rw", [P, DC, 2 * E], F32R)
        rw_raw = sb("rw_raw", [P, DC, E])
        W1 = [[sb(f"W1_{p}{v}", [P, DC, H], F32R) for p in ("hi", "lo")] for v in range(2)]
        W2 = [[sb(f"W2_{p}{v}", [P, HC, D], F32R) for p in ("hi", "lo")] for v in range(2)]
        bias_rows = sb("bias_rows", [P, P])
        biasT = sb("biasT", [P, P])
        neg_bg = sb("neg_bg", [P, DC])
        bo_b = sb("bo_b", [P, D])
        ob2_b = sb("ob2_b", [P, D])
        b2_b = sb("b2_b", [P, E, D])
        rb_b = sb("rb_b", [P, E])
        OB1 = E * HC
        BG = OB1 + HC

        ident = sb("ident", [P, P])
        upto = sb("upto", [P, P], BF16)
        ones = sb("ones", [P, P], BF16)
        first = sb("first", [P, E])
        row0 = sb("row0", [P, E])
        mhalf = sb("mhalf", [P, TG])
        zrow = sb("zrow", [P, ROW])
        warm = sb("warm", [P, 1])
        id_int = sb("id_int", [P, 2, TG], I32)

        xin = [sb(f"xin{v}", [P, TG, D]) for v in range(2)]
        xe = [xin[v][:].rearrange("p t d -> p (t d)")[:, 0:ET * PITCH].rearrange("p (t d) -> p t d", d=PITCH)
              for v in range(2)]
        tok = sb("tok", [P, TG, D])
        xnT = sb("xnT", [P, DC, GT])
        xnT_hi = sb("xnT_hi", [P, DC, GT], F32R)
        xnT_lo = sb("xnT_lo", [P, DC, GT], F32R)
        keep = sb("keep", [P, DC, GT])
        hst = [sb(f"hst{v}", [P, DC, GT]) for v in range(2)]
        hst_hi = sb("hst_hi", [P, DC, GT], F32R)
        hst_lo = sb("hst_lo", [P, DC, GT], F32R)
        att = sb("att", [P, TG, D])
        x1 = [sb(f"x1_{v}", [P, TG, PITCH]) for v in range(2)]
        tok2 = sb("tok2", [P, TG, D])
        xfT_hi = sb("xfT_hi", [P, DC, GT], F32R)
        xfT_lo = sb("xfT_lo", [P, DC, GT], F32R)
        hid = [sb(f"hid{v}", [P, GT]) for v in range(2)]
        hid_hi = [sb(f"hid_hi{r}", [P, GT], F32R) for r in range(4)]
        hid_lo = [sb(f"hid_lo{r}", [P, GT], F32R) for r in range(4)]
        ysb = sb("ysb", [P, TG, D])
        outt = [sb(f"outt{v}", [P, TG, D]) for v in range(2)]

        st = [sb(f"st{k}", [P, TG, 6]) for k in range(4)]
        mv = [sb(f"mv{k}", [P, TG, 2]) for k in range(4)]
        veps = [sb(f"veps{k}", [P, TG]) for k in range(4)]
        nmean = [sb(f"nmean{k}", [P, TG]) for k in range(4)]
        rstd = [sb(f"rstd{k}", [P, TG]) for k in range(4)]
        nmr = [sb(f"nmr{k}", [P, TG]) for k in range(4)]

        lgT = sb("lgT", [2 * E, GT])
        lg = [sb(f"lg{k}", [P, TG, E]) for k in range(3)]
        lmax = sb("lmax", [P, TG])
        cand = sb("cand", [P, TG, E])
        cmax = sb("cmax", [P, TG])
        oh = sb("oh", [P, TG, E], BF16)
        seen = sb("seen", [P, E], BF16)
        seen_g = sb("seen_g", [P, E])
        rk = [sb(f"rk{k}", [P, TG, E]) for k in range(4)]
        slot = sb("slot", [P, TG])
        idx = [sb(f"idx{v}", [P, TG], I32) for v in range(2)]
        oidx = [sb(f"oidx{v}", [P, ET], I32) for v in range(2)]

        psT = ctx.enter_context(nc.psum_tensor("psT", [P, DC, GT], F32))
        psA = ctx.enter_context(nc.psum_tensor("psA", [P, 2, GT], F32))
        psH = ctx.enter_context(nc.psum_tensor("psH", [P, 2, GT], F32))
        psY = ctx.enter_context(nc.psum_tensor("psY", [P, 2, GT], F32))
        psA_t = psA[:].rearrange("p a (t d) -> p (a t) d", d=D)
        psY_t = psY[:].rearrange("p a (t d) -> p (a t) d", d=D)
        logitsT = psT[0:2 * E, 0, :]
        logits = psT[:, 1, 0:TG * 2 * E].rearrange("p (t e) -> p t e", t=TG)
        ranks = psA[:, 1, 0:TG * E].rearrange("p (t e) -> p t e", t=TG)

        s_x_in = sems("s_x_in")
        s_xbuf0 = sem("s_xbuf0")
        s_w = {n: sem(f"s_w_{n}") for n in ("wg", "wo", "rw", "ow", "bias", "bcast", "b2")}
        s_const = sem("s_const")
        s_held = sem("s_held")
        s_held_pe = sem("s_held_pe")
        s_held_v = sem("s_held_v")
        s_pc = sem("s_pc")
        s_id = sem("s_id")
        s_bias_z = sem("s_bias_z")
        s_warm = sem("s_warm")
        s_wT = sem("s_wT")
        s_wT_hi = sem("s_wT_hi")
        s_wT_lo = sem("s_wT_lo")
        s_rw_hi = sem("s_rw_hi")
        s_rw_lo = sem("s_rw_lo")
        s_ow_hi = sem("s_ow_hi")
        s_ow_lo = sem("s_ow_lo")
        s_biasT = sem("s_biasT")
        s_st = [sem(f"s_st{k}") for k in range(4)]
        s_ag = [sem(f"s_ag{k}") for k in range(4)]
        s_ve = [sem(f"s_ve{k}") for k in range(4)]
        s_rs = [sem(f"s_rs{k}") for k in range(4)]
        s_nm = [sem(f"s_nm{k}") for k in range(4)]
        s_tok = sem("s_tok")
        s_T0 = sem("s_T0")
        s_xn_hi = sem("s_xn_hi")
        s_xn_lo = sem("s_xn_lo")
        s_gate = sem("s_gate")
        s_keep = sem("s_keep")
        s_ngx = sem("s_ngx")
        s_scan = sem("s_scan")
        s_h_hi = sem("s_h_hi")
        s_h_lo = sem("s_h_lo")
        s_wo = sem("s_wo")
        s_att = sem("s_att")
        s_u = sem("s_u")
        s_x1 = sem("s_x1")
        s_tok2 = sem("s_tok2")
        s_T1 = sem("s_T1")
        s_xf_hi = sem("s_xf_hi")
        s_xf_lo = sem("s_xf_lo")
        s_lgT = sem("s_lgT")
        s_lgT_sb = sem("s_lgT_sb")
        s_lg = sem("s_lg")
        s_rt = sem("s_rt")
        s_oh = sem("s_oh")
        s_rank = sem("s_rank")
        s_sl = sem("s_sl")
        s_idx = sem("s_idx")
        s_seen = sem("s_seen")
        s_scat = sems("s_scat")
        s_l1 = sem("s_l1")
        s_hid = sem("s_hid")
        s_hid_hi = sem("s_hid_hi")
        s_hid_lo = sem("s_hid_lo")
        s_l2 = sem("s_l2")
        s_y = sem("s_y")
        s_z = sem("s_z")
        s_out = sem("s_out")
        s_st_out = sems("s_st_out")
        s_we = [sems(f"s_we{m}_") for m in (1, 2)]
        s_we_hi = sem("s_we_hi")
        s_we_lo = sem("s_we_lo")
        s_xe = sems("s_xe")
        s_oidx = sem("s_oidx")
        s_pre = sem("s_pre")
        s_fin = sems("s_fin")

        EL1 = cnt((NG // 2, 0), HC, 0)

        block = ctx.enter_context(nc.Block())

        def stage_w1():
            return stage[:, 0, :].rearrange("p (c h) -> p c h", c=DC)

        def stage_w2():
            return stage[:, 1, :].rearrange("p (c d) -> p c d", c=HC)

        @block.sync
        def _(sp):
            def load(g):
                i, v = g
                sp.dma_start(xin[v][:], x[i, v * GT:(v + 1) * GT, :].rearrange("(t p) d -> p t d", p=P))\
                    .then_inc(s_x_in[v], 16)

            load((0, 0))
            wg_raw = outt[0][:, 0:DC, :]
            wo_raw = outt[1][:, 0:DC, :]
            sp.dma_start(wg_raw, Wg.rearrange("(c p) d -> p c d", p=P)).then_inc(s_w["wg"], 16)
            sp.dma_start(wo_raw, Wo.rearrange("(c p) d -> p c d", p=P)).then_inc(s_w["wo"], 16)
            sp.wait_ge(s_bias_z, 1)
            sp.dma_start(bias_rows[0:OB1, :], b1.rearrange("e (j p) -> (e j) p", p=P)).then_inc(s_w["bias"], 16)
            sp.dma_start(bias_rows[OB1:BG, :], ob1.rearrange("(j p) -> j p", p=P)).then_inc(s_w["bias"], 16)
            sp.dma_start(bias_rows[BG:BG + DC, :], bg.rearrange("(j p) -> j p", p=P)).then_inc(s_w["bias"], 16)
            load((0, 1))
            for dst, src in ((bo_b[:], bo), (ob2_b[:], ob2), (rb_b[:], router_b)):
                sp.dma_start(dst, src.partition_broadcast(P)).then_inc(s_w["bcast"], 16)
            sp.dma_start(rw_raw[:], router_w.rearrange("(c p) e -> p c e", p=P)).then_inc(s_w["rw"], 16)
            sp.dma_start(stage_w1(), ow1.rearrange("(c p) h -> p c h", p=P)).then_inc(s_w["ow"], 16)
            sp.dma_start(stage_w2(), ow2.rearrange("(c p) d -> p c d", p=P)).then_inc(s_w["ow"], 16)
            sp.dma_start(b2_b[:], b2.partition_broadcast(P)).then_inc(s_w["b2"], 16)
            sp.wait_ge(s_const, 1)
            sp.dma_start(xbuf.rearrange("(n p) c -> p n c", p=P),
                         zrow[:].unsqueeze(1).to_broadcast([P, E * C // P, ROW])).then_inc(s_xbuf0, 16)

            def load_w1(e):
                i, v = e
                sp.dma_start(stage_w1(), w1[i * 2 + v].rearrange("(c p) h -> p c h", p=P)).then_inc(s_we[0][v], 16)

            def load_w2(e):
                i, v = e
                sp.dma_start(stage_w2(), w2[i * 2 + v].rearrange("(c p) d -> p c d", p=P)).then_inc(s_we[1][v], 16)

            def store(g):
                i, v = g
                sp.wait_ge(s_out, cnt(g, 1, 1))
                sp.dma_start(out[i, v * GT:(v + 1) * GT, :].rearrange("(t p) d -> p t d", p=P), outt[v][:])\
                    .then_inc(s_st_out[v], 16)

            def step(i, u):
                prev, nxt, far = grp(i, u, -1), grp(i, u, 1), grp(i, u, 3)
                if live(prev, NG):
                    store(prev)
                if live(far, NG):
                    sp.wait_ge(s_x1, cnt(nxt, 1, 1))
                    load(far)

            sp.wait_ge(s_x1, 1)
            load((1, 0))
            sp.wait_ge(s_ow_hi, 4)
            sp.wait_ge(s_ow_lo, 4)
            load_w1((0, 0))
            load_w2((0, 0))
            for u in range(2):
                step(0, u)
            with sp.Fori(1, NG // 2 - 2) as i:
                for u in range(2):
                    step(i, u)
            for u in range(4):
                step(*grp(NG // 2 - 2, u, 0))
            def load_rows(e):
                i, v = e
                ei = i * 2 + v
                rows = xbuf.rearrange("(e c) w -> e c w", c=C)[ei]
                full = (C // P) * P
                sp.dma_start(xe[v][:, 0:C // P, 0:ROW], rows[0:full].rearrange("(t p) c -> p t c", p=P))\
                    .then_inc(s_xe[v], 16)
                sp.dma_start(xe[v][0:C - full, C // P, 0:ROW], rows[full:C]).then_inc(s_xe[v], 16)

            sp.wait_ge(s_we_hi, 4)
            sp.wait_ge(s_we_lo, 4)
            load_w1((0, 1))
            for v in range(2):
                sp.wait_ge(s_scat[v], landed((NG // 2 - 1, 0), TG))
            for v in range(2):
                load_rows((0, v))
            sp.wait_ge(s_we_hi, 8)
            sp.wait_ge(s_we_lo, 8)
            load_w2((0, 1))
            store((NG // 2 - 1, 1))

            def estep(i, u):
                now, nxt, far = grp(i, u, 0), grp(i, u, 1), grp(i, u, 2)
                sp.wait_ge(s_pre, cnt(now, 1, 1))
                load_rows(far)
                sp.wait_ge(s_we_hi, cnt(nxt, 8, 4))
                sp.wait_ge(s_we_lo, cnt(nxt, 8, 4))
                load_w1(far)
                sp.wait_ge(s_we_hi, cnt(nxt, 8, 8))
                sp.wait_ge(s_we_lo, cnt(nxt, 8, 8))
                load_w2(far)

            for u in range(2):
                estep(0, u)
            with sp.Fori(1, E // 2 - 1) as i:
                for u in range(2):
                    estep(i, u)

        @block.gpsimd
        def _(pool):
            pool.memset(ident[:], 0.0).then_inc(s_pc, 1)
            pool.memset(upto[:], 1.0).then_inc(s_pc, 1)
            pool.memset(ones[:], 1.0)
            pool.memset(mhalf[:], -0.5)
            pool.memset(zrow[:], 0.0).then_inc(s_pc, 1)
            pool.wait_ge(s_pc, 3)
            pool.affine_select(out=ident[:], in_=ident[:], compare_op=ALU.not_equal, fill=1.0, base=0,
                               pattern=[[-1, P]], channel_multiplier=1)
            pool.affine_select(out=upto[:], in_=upto[:], compare_op=ALU.is_ge, fill=0.0, base=0,
                               pattern=[[1, P]], channel_multiplier=-1)
            pool.memset(zrow[:, D:ROW], NOWHERE)
            pool.iota(first[:], pattern=[[-1, E]], base=E, channel_multiplier=0, allow_small_or_imprecise_dtypes=True)
            pool.iota(row0[:], pattern=[[C, E]], base=-1, channel_multiplier=0, allow_small_or_imprecise_dtypes=True)
            pool.iota(id_int[:], pattern=[[GT, 2], [P, TG]], base=0, channel_multiplier=1).then_inc(s_const, 1)
            pool.wait_ge(s_const, 1)
            for v in range(2):
                pool.tensor_copy(x1[v][:, :, D:ROW], id_int[:, v, :].unsqueeze(2)).then_inc(s_id, 1)

            def deviation(k, g, n, extra=0):
                pool.wait_ge(s_ve[k], cnt(g, 1, 1) + extra)
                pool.tensor_tensor(rstd[k][:, 0:n], veps[k][:, 0:n], mhalf[:, 0:n], ALU.pow).then_inc(s_rs[k], 1)
                pool.wait_ge(s_rs[k], cnt(g, 1, 1) + extra)
                pool.tensor_tensor(nmr[k][:, 0:n], nmean[k][:, 0:n], rstd[k][:, 0:n], ALU.mult).then_inc(s_nm[k], 1)

            def norm0(g):
                i, v = g
                deviation(0, g, TG)
                pool.wait_ge(s_nm[0], cnt(g, 1, 1))
                pool.wait_ge(s_T0, cnt(g, 2, 0))
                pool.sem_inc(s_held, 1)
                for t in range(TG):
                    last = pool.tensor_scalar(tok[:, t, :], xin[v][:, t, :], rstd[0][:, t:t + 1], nmr[0][:, t:t + 1],
                                              ALU.mult, ALU.add)
                last.then_inc(s_tok, 1)

            def dispatch(g, tiles):
                i, v = g
                pool.wait_ge(s_idx, cnt(g, 1, 1))
                pool.sem_inc(s_held, 1)
                for t in tiles:
                    pool.indirect_dma_start(out=xbuf, out_offset=bass.IndirectOffsetOnAxis(idx[v][:, t:t + 1], 0),
                                            in_=x1[v][:, t, 0:ROW], in_offset=None, bounds_check=E * C - 1,
                                            oob_is_err=False).then_inc(s_scat[v], 16)

            def renumber(g):
                i, v = g
                if live(grp(i, v, -2), NG):
                    pool.wait_ge(s_scat[v], landed(grp(i, v, -2), TG))
                    pool.sem_inc(s_held, 1)
                    pool.tensor_scalar(x1[v][:, :, D:ROW], x1[v][:, :, D:ROW], float(2 * GT), None, ALU.add)\
                        .then_inc(s_id, 1)

            def norm2(g, src, n, base=0):
                i, v = g
                deviation(2, g, n, base)
                pool.wait_ge(s_nm[2], cnt(g, 1, 1) + base)
                pool.wait_ge(s_T1, cnt(g, 2, 0) + 2 * base)
                pool.sem_inc(s_held, 1)
                for t in range(n):
                    last = pool.tensor_scalar(tok2[:, t, :], src[v][:, t, 0:D], rstd[2][:, t:t + 1],
                                              nmr[2][:, t:t + 1], ALU.mult, ALU.add)
                last.then_inc(s_tok2, 1)

            def state_lo(g):
                i, v = g
                pool.wait_ge(s_wo, cnt(g, 2, 0))
                for c in range(DC):
                    pool.wait_ge(s_h_hi, cnt(g, 2, c + 1))
                    pool.tensor_tensor(hst_lo[:, c, :], hst[v][:, c, :], hst_hi[:, c, :].bitcast(F32), ALU.subtract)\
                        .then_inc(s_h_lo, 1)

            def step(i, u):
                prev, now, nxt, far = grp(i, u, -1), grp(i, u, 0), grp(i, u, 1), grp(i, u, 2)
                if live(prev, NG):
                    deviation(3, prev, TG)
                if live(far, NG):
                    norm0(far)
                if live(prev, NG):
                    residual2(prev)
                if live(nxt, NG):
                    deviation(1, nxt, TG)
                    renumber(nxt)
                if live(now, NG):
                    dispatch(now, range(TG))
                if live(nxt, NG):
                    norm2(nxt, x1, TG)
                if live(far, NG):
                    state_lo(far)

            def residual2(g):
                i, v = g
                pool.wait_ge(s_z, cnt(g, 1, 1))
                if live(grp(i, v, -2), NG):
                    pool.wait_ge(s_st_out[v], landed(grp(i, v, -2)))
                pool.tensor_tensor(outt[v][:], ysb[:], x1[v][:, :, 0:D], ALU.add).then_inc(s_out, 1)

            norm0((0, 0))
            pool.wait_ge(s_tok, 1)
            norm0((0, 1))
            state_lo((0, 0))
            deviation(1, (0, 0), TG)
            norm2((0, 0), x1, TG)
            state_lo((0, 1))
            pool.wait_ge(s_xbuf0, 16)
            for u in range(2):
                step(0, u)
            with pool.Fori(1, NG // 2 - 1) as i:
                for u in range(2):
                    step(i, u)
            for u in range(2):
                step(NG // 2 - 1, u)

            def keep_rows(e):
                i, v = e
                if live(grp(i, v, -2), E):
                    pool.wait_ge(s_out, cnt(grp(i, v, -2), 1, 1) + NG)
                    pool.wait_ge(s_oidx, cnt(grp(i, v, -2), 1, 1))
                else:
                    pool.wait_ge(s_scat[v], landed((NG // 2 - 1, v), TG))
                    pool.wait_ge(s_out, cnt((NG // 2 - 1, v), 1, 1))
                pool.sem_inc(s_held, 1)
                pool.tensor_copy(x1[v][:, 0:ET, 0:ROW], xe[v][:, 0:ET, 0:ROW]).then_inc(s_pre, 1)

            def residual3(e):
                i, v = e
                pool.wait_ge(s_pre, cnt(e, 1, 1))
                pool.wait_ge(s_z, cnt(e, 1, 1) + NG)
                if live(grp(i, v, -2), E):
                    pool.wait_ge(s_fin[v], landed(grp(i, v, -2), ET))
                pool.sem_inc(s_held, 1)
                pool.tensor_tensor(outt[v][:, 0:ET, :], ysb[:, 0:ET, :], x1[v][:, 0:ET, 0:D], ALU.add)\
                    .then_inc(s_out, 1)
                pool.tensor_copy(oidx[v][:].unsqueeze(2), x1[v][:, 0:ET, D:ROW]).then_inc(s_oidx, 1)

            def store_rows(e):
                i, v = e
                pool.wait_ge(s_out, cnt(e, 1, 1) + NG)
                pool.wait_ge(s_oidx, cnt(e, 1, 1))
                pool.sem_inc(s_held, 1)
                for t in range(ET):
                    n = min(P, C - t * P)
                    pool.indirect_dma_start(out=out_rows, out_offset=bass.IndirectOffsetOnAxis(oidx[v][0:n, t:t + 1], 0),
                                            in_=outt[v][0:n, t, :], in_offset=None, bounds_check=N - 1,
                                            oob_is_err=False).then_inc(s_fin[v], 16)

            def estep(i, u):
                prev, nxt = grp(i, u, -1), grp(i, u, 1)
                if live(prev, E):
                    deviation(3, prev, ET, NG)
                if live(nxt, E):
                    norm2(nxt, xe, ET, NG)
                if live(prev, E):
                    residual3(prev)
                if live(nxt, E):
                    keep_rows(nxt)
                if live(prev, E):
                    store_rows(prev)

            last_group, last_expert = (NG // 2 - 1, 1), (E // 2 - 1, 1)
            norm2((0, 0), xe, ET, NG)
            keep_rows((0, 0))
            deviation(3, last_group, TG)
            norm2((0, 1), xe, ET, NG)
            residual2(last_group)
            keep_rows((0, 1))
            for v in range(2):
                pool.wait_ge(s_st_out[v], landed((NG // 2 - 1, 0)))
            estep(0, 1)
            with pool.Fori(1, E // 2 - 1) as i:
                for u in range(2):
                    estep(i, u)
            for u in range(2):
                estep(E // 2 - 1, u)
            deviation(3, last_expert, ET, NG)
            residual3(last_expert)
            store_rows(last_expert)
            for v in range(2):
                pool.wait_ge(s_fin[v], landed((E // 2 - 1, 0), ET))

        @block.scalar
        def _(act):
            act.wait_ge(s_warm, 1)
            act.activation(warm[:], warm[:], ACT.Sigmoid)
            for n, W in enumerate((WgT, WoT)):
                act.wait_ge(s_wT, n + 1)
                act.activation(W[0][:], psA_t[:, 2 * n:2 * n + 2, :], ACT.Copy).then_inc(s_wT_hi, 1)
            act.wait_ge(s_wT, 3)
            act.activation(biasT[:], psH[:, 0, 0:P], ACT.Copy).then_inc(s_biasT, 1)

            def relu(g, j, n, bias, base=0):
                act.wait_ge(s_l1, cnt(g, HC, j + 1) + base)
                act.wait_ge(s_hid_lo, cnt(g, HC, max(j - 1, 0)) + base)
                act.activation(hid[j % 2][:, 0:n], psH[:, j % 2, 0:n], ACT.Relu, bias=bias).then_inc(s_hid, 1)
                act.wait_ge(s_hid, cnt(g, HC, j + 1) + base)
                act.wait_ge(s_l2, cnt(g, HC, max(j - 3, 0)) + base)
                act.activation(hid_hi[j % 4][:, 0:n], hid[j % 2][:, 0:n], ACT.Copy).then_inc(s_hid_hi, 1)

            def norm1(g):
                act.wait_ge(s_nm[1], cnt(g, 1, 1))
                act.wait_ge(s_att, cnt(g, 2, 2))
                for t in range(TG):
                    last = act.activation(att[:, t, :], att[:, t, :], ACT.Identity, bias=nmr[1][:, t:t + 1],
                                          scale=rstd[1][:, t:t + 1])
                last.then_inc(s_u, 1)

            def norm3(g, n, base=0):
                act.wait_ge(s_nm[3], cnt(g, 1, 1) + base)
                act.wait_ge(s_y, cnt(g, 2, 2) + 2 * base)
                for t in range(n):
                    last = act.activation(ysb[:, t, :], ysb[:, t, :], ACT.Identity, bias=nmr[3][:, t:t + 1],
                                          scale=rstd[3][:, t:t + 1])
                last.then_inc(s_z, 1)

            def xn_hi(g):
                act.wait_ge(s_gate, cnt(g, 2, 0))
                act.wait_ge(s_scan, cnt(g, 2, 0))
                for c in range(DC):
                    act.wait_ge(s_T0, cnt(g, 2, c + 1))
                    act.activation(xnT[:, c, :], psT[:, c, :], ACT.Copy)
                    act.activation(xnT_hi[:, c, :], psT[:, c, :], ACT.Copy).then_inc(s_xn_hi, 1)

            def sigmoid(g):
                act.wait_ge(s_scan, cnt(g, 2, 0))
                for c in range(DC):
                    act.wait_ge(s_gate, cnt(g, 2, c + 1))
                    act.activation(keep[:, c, :], psA[:, c, :], ACT.Sigmoid, bias=neg_bg[:, c:c + 1], scale=-1.0)\
                        .then_inc(s_keep, 1)

            def state_hi(g):
                i, v = g
                act.wait_ge(s_wo, cnt(g, 2, 0))
                for c in range(DC):
                    act.wait_ge(s_scan, cnt(g, 2, c + 1))
                    act.activation(hst_hi[:, c, :], hst[v][:, c, :], ACT.Copy).then_inc(s_h_hi, 1)

            def xf_hi(g, n, base=0):
                act.wait_ge(s_l1, cnt(g, HC, 0) + HC * base)
                act.wait_ge(s_lgT, cnt(g, 1, 0) if not base else NG)
                for c in range(DC):
                    act.wait_ge(s_T1, cnt(g, 2, c + 1) + 2 * base)
                    act.activation(xfT_hi[:, c, 0:n], psT[:, c, 0:n], ACT.Copy).then_inc(s_xf_hi, 1)

            def logits_out(g):
                act.wait_ge(s_lgT, cnt(g, 1, 1))
                act.wait_ge(s_lg, cnt(g, 1, 0))
                act.activation(lgT[:], logitsT, ACT.Copy).then_inc(s_lgT_sb, 1)

            def weights_hi(e, j):
                i, v = e
                m, q = j // 4, j % 4
                if q == 0:
                    act.wait_ge(s_we[m][v], landed(e))
                dst = (W1, W2)[m][v][0][:].rearrange("p a b -> p (a b)")
                act.activation(dst[:, q * 512:(q + 1) * 512], stage[:, m, q * 512:(q + 1) * 512], ACT.Copy)\
                    .then_inc(s_we_hi, 1)

            def step(i, u):
                now, nxt, far = grp(i, u, 0), grp(i, u, 1), grp(i, u, 2)
                run, up, ahead = live(now, NG), live(nxt, NG), live(far, NG)

                def hidden(js):
                    if run:
                        for j in js:
                            relu(now, j, GT, biasT[:, OB1 + j:OB1 + j + 1])

                hidden(range(0, 1))
                if run:
                    logits_out(now)
                hidden(range(1, 2))
                if live(grp(i, u, -1), NG):
                    norm3(grp(i, u, -1), TG)
                hidden(range(2, 4))
                if ahead:
                    xn_hi(far)
                hidden(range(4, 5))
                if up:
                    norm1(nxt)
                if not ahead:
                    for j in range(4 * u, 4 * u + 4):
                        weights_hi((0, 0), j)
                hidden(range(5, 6))
                if ahead:
                    sigmoid(far)
                hidden(range(6, 8))
                if up:
                    xf_hi(nxt, GT)
                if ahead:
                    state_hi(far)

            xn_hi((0, 0))
            act.wait_ge(s_biasT, 2)
            sigmoid((0, 0))
            state_hi((0, 0))
            act.wait_ge(s_w["rw"], 16)
            act.activation(rw[:, :, 0:E], rw_raw[:], ACT.Copy).then_inc(s_rw_hi, 1)
            xn_hi((0, 1))
            act.wait_ge(s_w["ow"], 32)
            for m, W in enumerate((W1, W2)):
                for q in range(2):
                    dst = W[1][0][:].rearrange("p a b -> p (a b)")
                    act.activation(dst[:, q * 1024:(q + 1) * 1024], stage[:, m, q * 1024:(q + 1) * 1024], ACT.Copy)\
                        .then_inc(s_ow_hi, 1)
            norm1((0, 0))
            sigmoid((0, 1))
            xf_hi((0, 0), GT)
            state_hi((0, 1))
            for u in range(2):
                step(0, u)
            with act.Fori(1, NG // 2 - 1) as i:
                for u in range(2):
                    step(i, u)
            for u in range(2):
                step(NG // 2 - 1, u)

            def estep(i, u):
                prev, now, nxt = grp(i, u, -1), grp(i, u, 0), grp(i, u, 1)
                more = live(nxt, E)
                for j in range(HC):
                    col = (now[0] * 2 + now[1]) * HC + j
                    relu(now, j, C, biasT[:, bass.ds(col, 1)], EL1)
                    if j == 3:
                        if live(prev, E):
                            norm3(prev, ET, NG)
                        else:
                            norm3((NG // 2 - 1, 1), TG)
                    if more:
                        if j == 0:
                            act.wait_ge(s_l2, cnt(now, HC, 0) + EL1)
                        if j == HC - 1:
                            xf_hi(nxt, C, NG)
                        weights_hi(nxt, j)

            xf_hi((0, 0), C, NG)
            for u in range(2):
                estep(0, u)
            with act.Fori(1, E // 2 - 1) as i:
                for u in range(2):
                    estep(i, u)
            for u in range(2):
                estep(E // 2 - 1, u)
            norm3((E // 2 - 1, 1), ET, NG)

        @block.vector
        def _(dve):
            dve.memset(bias_rows[:], 0.0).then_inc(s_bias_z, 1)
            dve.memset(seen[:], 0.0).then_inc(s_seen, 1)
            dve.memset(warm[:], 0.0).then_inc(s_warm, 1)

            def read_rows(k, src, n):
                for t in range(n):
                    last = dve.bn_stats(st[k][:, t, :], src(t))
                last.then_inc(s_st[k], 1)

            def moments(k, g, n, base=0):
                dve.wait_ge(s_st[k], cnt(g, 1, 1) + base)
                dve.sem_inc(s_held_v, 1)
                for t in range(n):
                    last = dve.bn_aggr(mv[k][:, t, :], st[k][:, t, :])
                last.then_inc(s_ag[k], 1)
                dve.wait_ge(s_nm[k], cnt(g, 1, 0) + base)
                dve.wait_ge(s_ag[k], cnt(g, 1, 1) + base)
                dve.tensor_scalar(veps[k][:, 0:n].unsqueeze(2), mv[k][:, 0:n, 1:2], EPS, None, ALU.add)
                dve.tensor_scalar(nmean[k][:, 0:n].unsqueeze(2), mv[k][:, 0:n, 0:1], -1.0, None, ALU.mult)\
                    .then_inc(s_ve[k], 1)

            def stats(k, src, g, n, base=0):
                read_rows(k, src, n)
                moments(k, g, n, base)

            def read_rows0(g):
                i, v = g
                dve.wait_ge(s_x_in[v], landed(g))
                read_rows(0, lambda t: xin[v][:, t, :], TG)

            def stats0(g):
                read_rows0(g)
                moments(0, g, TG)

            def xn_lo(g):
                dve.wait_ge(s_gate, cnt(g, 2, 0))
                for c in range(DC):
                    dve.wait_ge(s_xn_hi, cnt(g, 2, c + 1))
                    dve.tensor_tensor(xnT_lo[:, c, :], xnT[:, c, :], xnT_hi[:, c, :].bitcast(F32), ALU.subtract)\
                        .then_inc(s_xn_lo, 1)

            def recurrence(g):
                i, v = g
                if live(grp(i, v, -2), NG):
                    dve.wait_ge(s_h_lo, cnt(grp(i, v, -2), 2, 2))
                for c in range(DC):
                    dve.wait_ge(s_keep, cnt(g, 2, c + 1))
                    dve.scalar_tensor_tensor(out=xnT[:, c, :], in0=keep[:, c, :], scalar=-1.0, in1=xnT[:, c, :],
                                             op0=ALU.add, op1=ALU.mult).then_inc(s_ngx, 1)
                    if v == 1:
                        dve.wait_ge(s_scan, cnt(g, 2, 0))
                    dve.wait_ge(s_ngx, cnt(g, 2, c + 1))
                    carry = hst[0][:, c, GT - 1:GT] if v == 1 else 0.0
                    dve.tensor_tensor_scan(hst[v][:, c, :], keep[:, c, :], xnT[:, c, :], carry, ALU.mult,
                                           ALU.subtract).then_inc(s_scan, 1)

            def attended(g):
                for a in range(2):
                    dve.wait_ge(s_wo, cnt(g, 2, a + 1))
                    dve.tensor_tensor(att[:, 2 * a:2 * a + 2, :], psA_t[:, 2 * a:2 * a + 2, :],
                                      bo_b[:].unsqueeze(1).to_broadcast([P, 2, D]), ALU.add).then_inc(s_att, 1)

            def stats1(g):
                dve.wait_ge(s_att, cnt(g, 2, 2))
                stats(1, lambda t: att[:, t, :], g, TG)

            def residual1(g):
                i, v = g
                if live(grp(i, v, -2), NG):
                    dve.wait_ge(s_scat[v], landed(grp(i, v, -2), TG))
                    dve.wait_ge(s_out, cnt(grp(i, v, -2), 1, 1))
                dve.wait_ge(s_u, cnt(g, 1, 1))
                dve.tensor_tensor(x1[v][:, :, 0:D], att[:], xin[v][:], ALU.add).then_inc(s_x1, 1)

            def stats2(g):
                dve.wait_ge(s_x1, cnt(g, 1, 1))
                stats(2, lambda t: x1[g[1]][:, t, 0:D], g, TG)

            def xf_lo(g, n, base=0):
                for c in range(DC):
                    dve.wait_ge(s_xf_hi, cnt(g, 2, c + 1) + 2 * base)
                    dve.tensor_tensor(xfT_lo[:, c, 0:n], psT[:, c, 0:n], xfT_hi[:, c, 0:n].bitcast(F32),
                                      ALU.subtract).then_inc(s_xf_lo, 1)

            def choose(g):
                def link(n):
                    dve.wait_ge(s_rt, cnt(g, 6, n))

                dve.wait_ge(s_lg, cnt(g, 1, 1))
                dve.tensor_tensor(lg[0][:], logits[:, :, 0:E], rb_b[:].unsqueeze(1).to_broadcast([P, TG, E]), ALU.add)\
                    .then_inc(s_rt, 1)
                link(1)
                dve.tensor_tensor(lg[1][:], logits[:, :, E:2 * E], lg[0][:], ALU.add).then_inc(s_rt, 1)
                link(2)
                dve.tensor_reduce(lmax[:], lg[1][:], AX_X, ALU.max).then_inc(s_rt, 1)
                link(3)
                dve.tensor_tensor(lg[2][:], lg[1][:], lmax[:].unsqueeze(2).to_broadcast([P, TG, E]), ALU.subtract)\
                    .then_inc(s_rt, 1)
                link(4)
                dve.scalar_tensor_tensor(out=cand[:], in0=lg[2][:], scalar=-TIE,
                                         in1=first[:].unsqueeze(1).to_broadcast([P, TG, E]), op0=ALU.is_ge,
                                         op1=ALU.mult).then_inc(s_rt, 1)
                link(5)
                dve.tensor_reduce(cmax[:], cand[:], AX_X, ALU.max).then_inc(s_rt, 1)
                link(6)
                if live(grp(g[0], g[1], -1), NG):
                    dve.wait_ge(s_rank, cnt(g, 1, 0))
                dve.tensor_tensor(oh[:], cand[:], cmax[:].unsqueeze(2).to_broadcast([P, TG, E]), ALU.is_equal)\
                    .then_inc(s_oh, 1)

            def place(g):
                i, v = g

                def link(n):
                    dve.wait_ge(s_sl, cnt(g, 4, n))

                dve.wait_ge(s_rank, cnt(g, 1, 1))
                dve.tensor_tensor(rk[0][:], ranks, row0[:].unsqueeze(1).to_broadcast([P, TG, E]), ALU.add)
                dve.tensor_scalar(rk[1][:], ranks, C + 0.5, NOWHERE, ALU.is_ge, ALU.mult)
                dve.tensor_reduce(seen_g[:], oh[:].rearrange("p t e -> p e t"), AX_X, ALU.add).then_inc(s_sl, 1)
                link(1)
                dve.tensor_tensor(rk[2][:], rk[0][:], rk[1][:], ALU.add).then_inc(s_sl, 1)
                dve.tensor_tensor(seen[:], seen[:], seen_g[:], ALU.add).then_inc(s_seen, 1)
                link(2)
                dve.tensor_tensor(rk[3][:], rk[2][:], oh[:], ALU.mult).then_inc(s_sl, 1)
                link(3)
                dve.tensor_reduce(slot[:], rk[3][:], AX_X, ALU.add).then_inc(s_sl, 1)
                link(4)
                if live(grp(i, v, -2), NG):
                    dve.wait_ge(s_scat[v], landed(grp(i, v, -2), TG))
                dve.tensor_copy(idx[v][:], slot[:]).then_inc(s_idx, 1)

            def lo(g, j, n, base=0):
                dve.wait_ge(s_hid_hi, cnt(g, HC, j + 1) + base)
                dve.tensor_tensor(hid_lo[j % 4][:, 0:n], hid[j % 2][:, 0:n], hid_hi[j % 4][:, 0:n].bitcast(F32),
                                  ALU.subtract).then_inc(s_hid_lo, 1)

            def result(g, bias, n, base=0):
                dve.wait_ge(s_l2, cnt(g, HC, HC) + HC * base)
                if base or live(grp(g[0], g[1], -1), NG):
                    dve.wait_ge(s_out, cnt(g, 1, 0) + base)
                for a in range(2):
                    k = min(n - 2 * a, 2)
                    dve.tensor_tensor(ysb[:, 2 * a:2 * a + k, :], psY_t[:, 2 * a:2 * a + k, :],
                                      bias.to_broadcast([P, k, D]), ALU.add).then_inc(s_y, 1)

            def read_rows3(g, n, base=0):
                dve.wait_ge(s_y, cnt(g, 2, 2) + 2 * base)
                read_rows(3, lambda t: ysb[:, t, :], n)

            def stats3(g, n, base=0):
                read_rows3(g, n, base)
                moments(3, g, n, base)

            def weights_lo(e, j):
                i, v = e
                m, q = j // 4, j % 4
                hi = (W1, W2)[m][v][0][:].rearrange("p a b -> p (a b)")[:, q * 512:(q + 1) * 512]
                dst = (W1, W2)[m][v][1][:].rearrange("p a b -> p (a b)")[:, q * 512:(q + 1) * 512]
                dve.wait_ge(s_we_hi, cnt(e, 8, j + 1))
                dve.tensor_tensor(dst, stage[:, m, q * 512:(q + 1) * 512], hi.bitcast(F32), ALU.subtract)\
                    .then_inc(s_we_lo, 1)

            def read_rows2(e):
                i, v = e
                dve.wait_ge(s_xe[v], landed(e, 2))
                read_rows(2, lambda t: xe[v][:, t, 0:D], ET)

            def step(i, u):
                now, nxt, far = grp(i, u, 0), grp(i, u, 1), grp(i, u, 2)
                run, up, ahead = live(now, NG), live(nxt, NG), live(far, NG)

                def low(*js):
                    if run:
                        for j in js:
                            lo(now, j, GT)

                low(0, 1)
                if run:
                    choose(now)
                if up:
                    attended(nxt)
                low(2)
                if up:
                    stats1(nxt)
                low(3)
                if ahead:
                    xn_lo(far)
                if run:
                    place(now)
                low(4)
                if up:
                    residual1(nxt)
                    stats2(nxt)
                low(5)
                if ahead:
                    recurrence(far)
                else:
                    for j in range(4 * u, 4 * u + 4):
                        weights_lo((0, 0), j)
                low(6)
                next_x = grp(i, u, 3)
                if live(next_x, NG):
                    read_rows0(next_x)
                low(7)
                if up:
                    xf_lo(nxt, GT)
                if live(next_x, NG):
                    moments(0, next_x, TG)
                if run and not up:
                    read_rows2((0, 0))
                    moments(2, (0, 0), ET, NG)
                if run:
                    result(now, ob2_b[:].unsqueeze(1), TG)
                if run and not up:
                    xf_lo((0, 0), C, NG)
                if run:
                    stats3(now, TG)

            def overflow_lo(m):
                W = (W1, W2)[m]
                for q in range(2):
                    hi = W[1][0][:].rearrange("p a b -> p (a b)")[:, q * 1024:(q + 1) * 1024]
                    dst = W[1][1][:].rearrange("p a b -> p (a b)")[:, q * 1024:(q + 1) * 1024]
                    dve.wait_ge(s_ow_hi, 2 * m + q + 1)
                    dve.tensor_tensor(dst, stage[:, m, q * 1024:(q + 1) * 1024], hi.bitcast(F32), ALU.subtract)\
                        .then_inc(s_ow_lo, 1)

            stats0((0, 0))
            for n, W in enumerate((WgT, WoT)):
                dve.wait_ge(s_wT_hi, n + 1)
                dve.tensor_tensor(W[1][:], psA_t[:, 2 * n:2 * n + 2, :], W[0][:].bitcast(F32), ALU.subtract)\
                    .then_inc(s_wT_lo, 1)
            dve.wait_ge(s_biasT, 1)
            dve.tensor_scalar(neg_bg[:], biasT[:, BG:BG + DC], -1.0, None, ALU.mult).then_inc(s_biasT, 1)
            stats0((0, 1))
            xn_lo((0, 0))
            recurrence((0, 0))
            dve.wait_ge(s_rw_hi, 1)
            dve.tensor_tensor(rw[:, :, E:2 * E], rw_raw[:], rw[:, :, 0:E].bitcast(F32), ALU.subtract).then_inc(s_rw_lo, 1)
            xn_lo((0, 1))
            dve.wait_ge(s_w["bcast"], 48)
            attended((0, 0))
            stats1((0, 0))
            overflow_lo(0)
            residual1((0, 0))
            stats2((0, 0))
            recurrence((0, 1))
            overflow_lo(1)
            xf_lo((0, 0), GT)
            stats0((1, 0))
            dve.wait_ge(s_w["b2"], 16)

            for u in range(2):
                step(0, u)
            with dve.Fori(1, NG // 2 - 2) as i:
                for u in range(2):
                    step(i, u)
            for u in range(4):
                step(*grp(NG // 2 - 2, u, 0))

            def estep(i, u):
                prev, now, nxt = grp(i, u, -1), grp(i, u, 0), grp(i, u, 1)
                for j in range(HC):
                    lo(now, j, C, EL1)
                    if j == 0 and live(prev, E):
                        read_rows3(prev, ET, NG)
                    if j == 1 and live(prev, E):
                        moments(3, prev, ET, NG)
                    if live(nxt, E):
                        if j == 2:
                            read_rows2(nxt)
                        if j == 3:
                            moments(2, nxt, ET, NG)
                        if j == HC - 1:
                            xf_lo(nxt, C, NG)
                        weights_lo(nxt, j)
                ei = now[0] * 2 + now[1]
                result(now, b2_b[:, bass.ds(ei, 1), :], ET, NG)

            for u in range(2):
                estep(0, u)
            with dve.Fori(1, E // 2 - 1) as i:
                for u in range(2):
                    estep(i, u)
            for u in range(2):
                estep(E // 2 - 1, u)
            stats3((E // 2 - 1, 1), ET, NG)

        @block.tensor
        def _(pe):
            pe.wait_ge(s_const, 1)
            for n, (name, raw) in enumerate((("wg", outt[0]), ("wo", outt[1]))):
                pe.wait_ge(s_w[name], 16)
                for c in range(DC):
                    for a in range(DC):
                        last = pe.transpose(psA_t[:, 2 * n + c, a * P:(a + 1) * P], raw[:, a, c * P:(c + 1) * P],
                                            ident[:])
                last.then_inc(s_wT, 1)
            pe.wait_ge(s_w["bias"], 48)
            pe.transpose(psH[:, 0, 0:P], bias_rows[:], ident[:]).then_inc(s_wT, 1)

            def split_product(dst, w, ws, r, rs, k, last_k):
                w_hi, w_lo = w[0][ws], w[1][ws]
                r_hi, r_lo = r[0][rs], r[1][rs]
                pe.matmul(dst, w_hi, r_hi, start=(k == 0), stop=False)
                pe.matmul(dst, w_hi, r_lo, start=False, stop=False)
                return pe.matmul(dst, w_lo, r_hi, start=False, stop=(k == last_k))

            ALL = slice(None)

            def transposes0(g):
                pe.wait_ge(s_tok, cnt(g, 1, 1))
                prev = grp(g[0], g[1], -2)
                if live(prev, NG):
                    pe.wait_ge(s_oh, cnt(prev, 1, 1))
                for c in range(DC):
                    for t in range(TG):
                        last = pe.transpose(psT[:, c, t * P:(t + 1) * P], tok[:, t, c * P:(c + 1) * P], ident[:])
                    last.then_inc(s_T0, 1)

            def gate(g):
                pe.wait_ge(s_xn_hi, cnt(g, 2, 2))
                pe.wait_ge(s_xn_lo, cnt(g, 2, 2))
                prev = grp(g[0], g[1], -1)
                if live(prev, NG):
                    pe.wait_ge(s_att, cnt(prev, 2, 2))
                prev = grp(g[0], g[1], -2)
                if live(prev, NG):
                    pe.wait_ge(s_idx, cnt(prev, 1, 1))
                for m in range(DC):
                    for k in range(DC):
                        last = split_product(psA[:, m, :], WgT, (ALL, k, slice(m * P, (m + 1) * P)),
                                             (xnT_hi, xnT_lo), (ALL, k, ALL), k, DC - 1)
                    last.then_inc(s_gate, 1)

            def project(g):
                pe.wait_ge(s_keep, cnt(g, 2, 2))
                pe.wait_ge(s_h_hi, cnt(g, 2, 2))
                pe.wait_ge(s_h_lo, cnt(g, 2, 2))
                for t in range(TG):
                    for k in range(DC):
                        last = split_product(psA_t[:, t, :], (hst_hi, hst_lo), (ALL, k, slice(t * P, (t + 1) * P)),
                                             WoT, (ALL, k, ALL), k, DC - 1)
                    if t % 2:
                        last.then_inc(s_wo, 1)

            def transposes1(g, n, base=0):
                pe.wait_ge(s_tok2, cnt(g, 1, 1) + base)
                if base == 0:
                    far = grp(g[0], g[1], 1)
                    if live(far, NG):
                        pe.wait_ge(s_xn_hi, cnt(far, 2, 2))
                    elif live(g, NG):
                        pe.wait_ge(s_oh, cnt(g, 1, 0))
                else:
                    pe.wait_ge(s_xf_lo, cnt(g, 2, 0) + 2 * base)
                    pe.wait_ge(s_xf_hi, cnt(g, 2, 0) + 2 * base)
                    pe.wait_ge(s_oh, NG)
                for c in range(DC):
                    for t in range(n):
                        last = pe.transpose(psT[:, c, t * P:(t + 1) * P], tok2[:, t, c * P:(c + 1) * P], ident[:])
                    last.then_inc(s_T1, 1)

            def route(g):
                for k in range(DC):
                    pe.matmul(logitsT, rw[:, k, :], xfT_hi[:, k, :], start=(k == 0), stop=False)
                for k in range(DC):
                    last = pe.matmul(logitsT[0:E], rw[:, k, 0:E], xfT_lo[:, k, :], start=False, stop=(k == DC - 1))
                last.then_inc(s_lgT, 1)

            def logits_by_token(g):
                pe.wait_ge(s_lgT_sb, cnt(g, 1, 1))
                pe.sem_inc(s_held_pe, 1)
                for t in range(TG):
                    last = pe.transpose(logits[:, t, :], lgT[:, t * P:(t + 1) * P], ident[0:2 * E, 0:2 * E])
                last.then_inc(s_lg, 1)

            def rank(g):
                if live(grp(g[0], g[1], 1), NG):
                    pe.wait_ge(s_att, cnt(g, 2, 4))
                pe.wait_ge(s_seen, cnt(g, 1, 1))
                pe.wait_ge(s_oh, cnt(g, 1, 1))
                pe.matmul(ranks, upto[:], oh[:], start=True, stop=False)
                pe.matmul(ranks, ones[:], seen[:].unsqueeze(1).to_broadcast([P, TG, E]), start=False, stop=False)
                for k in range(1, TG):
                    last = pe.matmul(ranks[:, k:TG, :], ones[:], oh[:, 0:TG - k, :], start=False, stop=(k == TG - 1))
                last.then_inc(s_rank, 1)

            def layer1(g, j, n, w, base=0):
                pe.wait_ge(s_hid, cnt(g, HC, max(j - 1, 0)) + base)
                for k in range(DC):
                    last = split_product(psH[:, j % 2, 0:n], w, (ALL, k, slice(j * P, (j + 1) * P)),
                                         (xfT_hi, xfT_lo), (ALL, k, slice(0, n)), k, DC - 1)
                last.then_inc(s_l1, 1)

            def layer2(g, j, n, w, base=0):
                pe.wait_ge(s_hid_lo, cnt(g, HC, j + 1) + base)
                for t in range(n):
                    tile = (ALL, slice(t * P, (t + 1) * P))
                    hi, lo_ = hid_hi[j % 4][tile], hid_lo[j % 4][tile]
                    pe.matmul(psY_t[:, t, :], hi, w[0][:, j, :], start=(j == 0 and t % 2 == 0), stop=False,
                              skip_group_check=True)
                    pe.matmul(psY_t[:, t, :], hi, w[1][:, j, :], start=False, stop=False, skip_group_check=True)
                    last = pe.matmul(psY_t[:, t, :], lo_, w[0][:, j, :], start=False, stop=(j == HC - 1),
                                     skip_group_check=True)
                last.then_inc(s_l2, 1)

            def step(i, u):
                now, nxt, far = grp(i, u, 0), grp(i, u, 1), grp(i, u, 2)
                run, up, ahead = live(now, NG), live(nxt, NG), live(far, NG)
                if run:
                    pe.wait_ge(s_xf_hi, cnt(now, 2, 2))
                    pe.wait_ge(s_xf_lo, cnt(now, 2, 2))
                    layer1(now, 0, GT, W1[1])
                    route(now)
                    layer1(now, 1, GT, W1[1])
                    logits_by_token(now)
                if up:
                    project(nxt)
                for j in range(2, HC):
                    if run:
                        layer1(now, j, GT, W1[1])
                        if j == 2 and live(grp(i, u, -1), NG):
                            pe.wait_ge(s_y, cnt(now, 2, 0))
                        if j == 4:
                            rank(now)
                        layer2(now, j - 2, TG, W2[1])
                    if j == 3 and ahead:
                        transposes0(far)
                    if j == 5 and ahead:
                        gate(far)
                if up:
                    transposes1(nxt, TG)
                if run:
                    layer2(now, HC - 2, TG, W2[1])
                    layer2(now, HC - 1, TG, W2[1])
                if not up:
                    transposes1((0, 0), ET, NG)

            transposes0((0, 0))
            pe.wait_ge(s_wT_lo, 2)
            gate((0, 0))
            transposes0((0, 1))
            project((0, 0))
            gate((0, 1))
            transposes1((0, 0), TG)
            pe.wait_ge(s_rw_lo, 1)
            pe.wait_ge(s_ow_lo, 4)
            for u in range(2):
                step(0, u)
            with pe.Fori(1, NG // 2 - 1) as i:
                for u in range(2):
                    step(i, u)
            for u in range(2):
                step(NG // 2 - 1, u)

            def estep(i, u):
                now, nxt = grp(i, u, 0), grp(i, u, 1)
                pe.wait_ge(s_we_lo, cnt(now, 8, 4))
                pe.wait_ge(s_xf_hi, cnt(now, 2, 2) + 2 * NG)
                pe.wait_ge(s_xf_lo, cnt(now, 2, 2) + 2 * NG)
                for j in range(HC + 2):
                    if j < HC:
                        layer1(now, j, C, W1[u], EL1)
                    if j == HC - 1 and live(nxt, E):
                        transposes1(nxt, ET, NG)
                    if j >= 2:
                        if j == 2:
                            pe.wait_ge(s_y, cnt(now, 2, 0) + 2 * NG)
                            pe.wait_ge(s_we_lo, cnt(now, 8, 8))
                        layer2(now, j - 2, ET, W2[u], EL1)

            for u in range(2):
                estep(0, u)
            with pe.Fori(1, E // 2 - 1) as i:
                for u in range(2):
                    estep(i, u)
            for u in range(2):
                estep(E // 2 - 1, u)


_INS = ["L0_attn_x", "L0_attn_Wg", "L0_attn_bg", "L0_attn_Wo", "L0_attn_bo", "L0_ffn_router_w", "L0_ffn_router_b",
        "L0_ffn_w1", "L0_ffn_b1", "L0_ffn_w2", "L0_ffn_b2", "L0_ffn_ow1", "L0_ffn_ob1", "L0_ffn_ow2", "L0_ffn_ob2"]


def kernel(**inputs):
    import numpy as np
    import concourse.bacc as bacc
    from concourse.bass_utils import run_bass_kernel_spmd

    nc = bacc.Bacc("TRN2", target_bir_lowering=False, num_devices=1)
    arrays, args = {}, []
    for name in _INS:
        a = np.ascontiguousarray(inputs[name])
        arrays[name] = a
        args.append(nc.dram_tensor(name, a.shape, mybir.dt.from_np(a.dtype), kind="ExternalInput").ap())
    args.append(nc.dram_tensor("out", arrays["L0_attn_x"].shape, F32, kind="ExternalOutput").ap())
    sandwich_kernel(nc, *args)
    r = run_bass_kernel_spmd(nc, [arrays], core_ids=[0])
    return r.results[0]["out"]
```
